# Optimizing a Trainium2 kernel written in Bass

```python
import numpy as np
import jax
import jax.numpy as jnp

def _softmax(x, axis=-1):
    return jax.nn.softmax(x, axis=axis)

def _gelu(x):
    return jax.nn.gelu(x, approximate=True)

def _silu(x):
    return jax.nn.silu(x)

def _sigmoid(x):
    return jax.nn.sigmoid(x)

def _layernorm(x, axis=-1, eps=1e-05):
    m = jnp.mean(x, axis=axis, keepdims=True)
    v = jnp.var(x, axis=axis, keepdims=True)
    return (x - m) / jnp.sqrt(v + eps)

def _scatter_add(tgt, idx, src, axis=0):
    return tgt.at[idx].add(src)

def _segment_sum(src, seg, n):
    return jax.ops.segment_sum(src, seg, n)
kernel_name = 'mk_audio_tower_d2_tok_audfeat256_r4_098c61'

def setup_inputs(seed: int=0):
    np.random.seed(seed)
    _w = jnp.asarray

    def _rec_inputs():
        import jax
        import jax.numpy as jnp
        _rk = jax.random.key(seed)
        x = -5.07413e-05 + 0.999912 * jax.random.normal(jax.random.fold_in(_rk, 1), (32, 375, 64), jnp.float32)
        return x
    x = _rec_inputs()

    def _L0_tok_setup():
        import jax, jax.numpy as jnp
        from jax import lax
        import numpy as np
        B, T, C, K, STRIDE = (16, 4000, 64, 5, 2)
        EPS = 0.001
        key = jax.random.key(seed)
        k0, k1, k2, k3 = jax.random.split(key, 4)
        x = jax.random.normal(k0, (B, T, C), dtype=jnp.float32)
        w = jax.random.normal(k1, (K, 1, C), dtype=jnp.float32) * 0.1
        b = jax.random.normal(k2, (C,), dtype=jnp.float32) * 0.01
        gamma = jnp.ones((C,), dtype=jnp.float32)
        beta = jnp.zeros((C,), dtype=jnp.float32)
        alpha = jnp.full((C,), 0.25, dtype=jnp.float32) + 0.01 * jax.random.normal(k3, (C,), dtype=jnp.float32)
        return {'x': x, 'w': w, 'b': b, 'gamma': gamma, 'beta': beta, 'alpha': alpha}
    _L0_tok_all = _L0_tok_setup()
    _L0_tok_in = {k: v for k, v in _L0_tok_all.items() if k in ('w', 'b', 'gamma', 'beta', 'alpha')}
    del _L0_tok_all

    def _L0_attn_setup():
        import jax, jax.numpy as jnp
        import numpy as np
        import math
        NUM_HEADS = 8
        HEAD_SIZE = 32

        def get_alibi_slopes(n_heads):

            def pow2_slopes(n):
                start = 2.0 ** (-2.0 ** (-(math.log2(n) - 3)))
                ratio = start
                return [start * ratio ** i for i in range(n)]
            if math.log2(n_heads).is_integer():
                return np.array(pow2_slopes(n_heads), dtype=np.float32)
            cp2 = 2 ** math.floor(math.log2(n_heads))
            extra = pow2_slopes(2 * cp2)[0::2][:n_heads - cp2]
            return np.array(pow2_slopes(cp2) + extra, dtype=np.float32)
        ALIBI_SLOPES = jnp.asarray(get_alibi_slopes(NUM_HEADS))
        key = jax.random.key(seed)
        ks = jax.random.split(key, 6)
        B, T, C = (32, 128, 64)
        s = 1.0 / math.sqrt(C)
        return {'x': jax.random.normal(ks[0], (B, T, C), dtype=jnp.float32), 'Wq': jax.random.normal(ks[1], (C, NUM_HEADS * HEAD_SIZE), dtype=jnp.float32) * s, 'Wk': jax.random.normal(ks[2], (C, NUM_HEADS * HEAD_SIZE), dtype=jnp.float32) * s, 'Wv': jax.random.normal(ks[3], (C, NUM_HEADS * HEAD_SIZE), dtype=jnp.float32) * s, 'Wo': jax.random.normal(ks[4], (NUM_HEADS * HEAD_SIZE, C), dtype=jnp.float32) * s, 'bo': jax.random.normal(ks[5], (C,), dtype=jnp.float32) * 0.01}
    _L0_attn_all = _L0_attn_setup()
    _L0_attn_in = {k: v for k, v in _L0_attn_all.items() if k in ('Wq', 'Wk', 'Wv', 'Wo', 'bo')}
    del _L0_attn_all

    def _L0_ffn_setup():
        import jax, jax.numpy as jnp
        import numpy as np
        B, S, H, NH, NE = (4, 256, 64, 4, 4)
        D = H // NH
        EPS = 1e-08

        def layernorm(x, g, b):
            m = jnp.mean(x, axis=-1, keepdims=True)
            v = jnp.mean((x - m) ** 2, axis=-1, keepdims=True)
            return (x - m) / jnp.sqrt(v + EPS) * g + b
        key = jax.random.key(seed)
        ks = jax.random.split(key, 18)
        sc = 0.05
        return {'x': jax.random.normal(ks[0], (B, S, H), jnp.float32), 'hl_w': jax.random.normal(ks[1], (NH, D, H), jnp.float32) * sc, 'hl_b': jax.random.normal(ks[2], (NH, D), jnp.float32) * sc, 'wq': jax.random.normal(ks[3], (NH, NE, D, D), jnp.float32) * sc, 'wk': jax.random.normal(ks[4], (NH, D, D), jnp.float32) * sc, 'wv': jax.random.normal(ks[5], (NH, D, D), jnp.float32) * sc, 'gate_w': jax.random.normal(ks[6], (NH, NE, NE * D), jnp.float32) * sc, 'gate_b': jax.random.normal(ks[7], (NH, NE), jnp.float32) * sc, 'ln_g': jnp.ones((D,), jnp.float32), 'ln_b': jnp.zeros((D,), jnp.float32), 'fc1_w': jax.random.normal(ks[8], (D, D), jnp.float32) * sc, 'fc1_b': jax.random.normal(ks[9], (D,), jnp.float32) * sc, 'fc2_w': jax.random.normal(ks[10], (D, D), jnp.float32) * sc, 'fc2_b': jax.random.normal(ks[11], (D,), jnp.float32) * sc, 'fnorm_g': jnp.ones((D,), jnp.float32), 'fnorm_b': jnp.zeros((D,), jnp.float32), 'fgate_w': jax.random.normal(ks[12], (NH, H), jnp.float32) * sc}
    _L0_ffn_all = _L0_ffn_setup()
    _L0_ffn_in = {k: v for k, v in _L0_ffn_all.items() if k in ('hl_w', 'hl_b', 'wq', 'wk', 'wv', 'gate_w', 'gate_b', 'ln_g', 'ln_b', 'fc1_w', 'fc1_b', 'fc2_w', 'fc2_b', 'fnorm_g', 'fnorm_b', 'fgate_w')}
    del _L0_ffn_all

    def _L1_attn_setup():
        import jax, jax.numpy as jnp
        import numpy as np
        A, Bc, Cc = (0.5, 1.0, 1.0)
        H = 8
        EPS = 1e-12

        def _normalize(t):
            n = jnp.linalg.norm(t, axis=-1, keepdims=True)
            return t / jnp.maximum(n, EPS)
        key = jax.random.key(seed)
        ks = jax.random.split(key, 5)
        B, N, C = (8, 512, 64)
        D = C // H
        x = jax.random.normal(ks[0], (B, N, C), dtype=jnp.float32)
        Wqkv = jax.random.normal(ks[1], (3 * H * D, C), dtype=jnp.float32) * 0.02
        bqkv = jnp.zeros((3 * H * D,), dtype=jnp.float32)
        Wproj = jax.random.normal(ks[2], (C, H * D), dtype=jnp.float32) * 0.02
        bproj = jnp.zeros((C,), dtype=jnp.float32)
        temperature = jnp.ones((1, H, 1, 1), dtype=jnp.float32)
        return {'x': x, 'Wqkv': Wqkv, 'bqkv': bqkv, 'Wproj': Wproj, 'bproj': bproj, 'temperature': temperature}
    _L1_attn_all = _L1_attn_setup()
    _L1_attn_in = {k: v for k, v in _L1_attn_all.items() if k in ('Wqkv', 'bqkv', 'Wproj', 'bproj', 'temperature')}
    del _L1_attn_all

    def _L1_ffn_setup():
        import jax, jax.numpy as jnp
        import numpy as np
        E = 8
        K = 2
        D = 64
        H = 128
        DOUT = 64
        EPS = 1e-05
        key = jax.random.key(seed)
        ks = jax.random.split(key, 9)
        s = 0.02
        return {'x': jax.random.normal(ks[0], (4, 2048, D), jnp.float32), 'gamma': 1.0 + 0.05 * jax.random.normal(ks[1], (D,), jnp.float32), 'beta': 0.05 * jax.random.normal(ks[2], (D,), jnp.float32), 'Wr': 0.01 * jax.random.normal(ks[3], (D, E), jnp.float32), 'br': jnp.zeros((E,), jnp.float32), 'W1': s * jax.random.normal(ks[4], (E, D, H), jnp.float32), 'b1': s * jax.random.normal(ks[5], (E, H), jnp.float32), 'W2': s * jax.random.normal(ks[6], (E, H, DOUT), jnp.float32), 'b2': s * jax.random.normal(ks[7], (E, DOUT), jnp.float32)}
    _L1_ffn_all = _L1_ffn_setup()
    _L1_ffn_in = {k: v for k, v in _L1_ffn_all.items() if k in ('gamma', 'beta', 'Wr', 'br', 'W1', 'b1', 'W2', 'b2')}
    del _L1_ffn_all
    return {'x': x, 'L0_tok_w': _L0_tok_in['w'], 'L0_tok_b': _L0_tok_in['b'], 'L0_tok_gamma': _L0_tok_in['gamma'], 'L0_tok_beta': _L0_tok_in['beta'], 'L0_tok_alpha': _L0_tok_in['alpha'], 'L0_attn_Wq': _L0_attn_in['Wq'], 'L0_attn_Wk': _L0_attn_in['Wk'], 'L0_attn_Wv': _L0_attn_in['Wv'], 'L0_attn_Wo': _L0_attn_in['Wo'], 'L0_attn_bo': _L0_attn_in['bo'], 'L0_ffn_hl_w': _L0_ffn_in['hl_w'], 'L0_ffn_hl_b': _L0_ffn_in['hl_b'], 'L0_ffn_wq': _L0_ffn_in['wq'], 'L0_ffn_wk': _L0_ffn_in['wk'], 'L0_ffn_wv': _L0_ffn_in['wv'], 'L0_ffn_gate_w': _L0_ffn_in['gate_w'], 'L0_ffn_gate_b': _L0_ffn_in['gate_b'], 'L0_ffn_ln_g': _L0_ffn_in['ln_g'], 'L0_ffn_ln_b': _L0_ffn_in['ln_b'], 'L0_ffn_fc1_w': _L0_ffn_in['fc1_w'], 'L0_ffn_fc1_b': _L0_ffn_in['fc1_b'], 'L0_ffn_fc2_w': _L0_ffn_in['fc2_w'], 'L0_ffn_fc2_b': _L0_ffn_in['fc2_b'], 'L0_ffn_fnorm_g': _L0_ffn_in['fnorm_g'], 'L0_ffn_fnorm_b': _L0_ffn_in['fnorm_b'], 'L0_ffn_fgate_w': _L0_ffn_in['fgate_w'], 'L1_attn_Wqkv': _L1_attn_in['Wqkv'], 'L1_attn_bqkv': _L1_attn_in['bqkv'], 'L1_attn_Wproj': _L1_attn_in['Wproj'], 'L1_attn_bproj': _L1_attn_in['bproj'], 'L1_attn_temperature': _L1_attn_in['temperature'], 'L1_ffn_gamma': _L1_ffn_in['gamma'], 'L1_ffn_beta': _L1_ffn_in['beta'], 'L1_ffn_Wr': _L1_ffn_in['Wr'], 'L1_ffn_br': _L1_ffn_in['br'], 'L1_ffn_W1': _L1_ffn_in['W1'], 'L1_ffn_b1': _L1_ffn_in['b1'], 'L1_ffn_W2': _L1_ffn_in['W2'], 'L1_ffn_b2': _L1_ffn_in['b2']}

def reference(x, L0_tok_w, L0_tok_b, L0_tok_gamma, L0_tok_beta, L0_tok_alpha, L0_attn_Wq, L0_attn_Wk, L0_attn_Wv, L0_attn_Wo, L0_attn_bo, L0_ffn_hl_w, L0_ffn_hl_b, L0_ffn_wq, L0_ffn_wk, L0_ffn_wv, L0_ffn_gate_w, L0_ffn_gate_b, L0_ffn_ln_g, L0_ffn_ln_b, L0_ffn_fc1_w, L0_ffn_fc1_b, L0_ffn_fc2_w, L0_ffn_fc2_b, L0_ffn_fnorm_g, L0_ffn_fnorm_b, L0_ffn_fgate_w, L1_attn_Wqkv, L1_attn_bqkv, L1_attn_Wproj, L1_attn_bproj, L1_attn_temperature, L1_ffn_gamma, L1_ffn_beta, L1_ffn_Wr, L1_ffn_br, L1_ffn_W1, L1_ffn_b1, L1_ffn_W2, L1_ffn_b2):
    import jax
    import jax.numpy as jnp

    def _L0_tok_ref(x, w, b, gamma, beta, alpha):
        import jax, jax.numpy as jnp
        from jax import lax
        import numpy as np
        B, T, C, K, STRIDE = (16, 4000, 64, 5, 2)
        EPS = 0.001
        y = lax.conv_general_dilated(x, w, window_strides=(STRIDE,), padding='SAME', dimension_numbers=('NWC', 'WIO', 'NWC'), feature_group_count=C) + b
        mean = jnp.mean(y, axis=(1, 2), keepdims=True)
        var = jnp.var(y, axis=(1, 2), keepdims=True)
        yn = (y - mean) * lax.rsqrt(var + EPS) * gamma + beta
        return jnp.where(yn > 0, yn, alpha * yn)

    def _L0_attn_ref(x, Wq, Wk, Wv, Wo, bo):
        import jax, jax.numpy as jnp
        import numpy as np
        import math
        NUM_HEADS = 8
        HEAD_SIZE = 32

        def get_alibi_slopes(n_heads):

            def pow2_slopes(n):
                start = 2.0 ** (-2.0 ** (-(math.log2(n) - 3)))
                ratio = start
                return [start * ratio ** i for i in range(n)]
            if math.log2(n_heads).is_integer():
                return np.array(pow2_slopes(n_heads), dtype=np.float32)
            cp2 = 2 ** math.floor(math.log2(n_heads))
            extra = pow2_slopes(2 * cp2)[0::2][:n_heads - cp2]
            return np.array(pow2_slopes(cp2) + extra, dtype=np.float32)
        ALIBI_SLOPES = jnp.asarray(get_alibi_slopes(NUM_HEADS))
        B, T, C = x.shape
        H, D = (NUM_HEADS, HEAD_SIZE)
        q = (x @ Wq).reshape(B, T, H, D).transpose(0, 2, 1, 3)
        k = (x @ Wk).reshape(B, T, H, D).transpose(0, 2, 1, 3)
        v = (x @ Wv).reshape(B, T, H, D).transpose(0, 2, 1, 3)
        scale = 1.0 / math.sqrt(D)
        wei = jnp.einsum('bhtd,bhsd->bhts', q, k) * scale
        pos = jnp.arange(T)
        rel = (pos[None, :] - pos[:, None]).astype(jnp.float32)
        bias = ALIBI_SLOPES[:, None, None] * rel[None, :, :]
        wei = wei + bias[None]
        causal = pos[None, :] <= pos[:, None]
        wei = jnp.where(causal[None, None], wei, -jnp.inf)
        wei = jax.nn.softmax(wei, axis=-1)
        out = jnp.einsum('bhts,bhsd->bhtd', wei, v)
        out = out.transpose(0, 2, 1, 3).reshape(B, T, H * D)
        return out @ Wo + bo

    def _L0_ffn_ref(x, hl_w, hl_b, wq, wk, wv, gate_w, gate_b, ln_g, ln_b, fc1_w, fc1_b, fc2_w, fc2_b, fnorm_g, fnorm_b, fgate_w):
        import jax, jax.numpy as jnp
        import numpy as np
        B, S, H, NH, NE = (4, 256, 64, 4, 4)
        D = H // NH
        EPS = 1e-08

        def layernorm(x, g, b):
            m = jnp.mean(x, axis=-1, keepdims=True)
            v = jnp.mean((x - m) ** 2, axis=-1, keepdims=True)
            return (x - m) / jnp.sqrt(v + EPS) * g + b
        b, s, h = x.shape
        nh, d, _ = wk.shape
        ne = wq.shape[1]
        sx = jnp.einsum('bsh,ndh->bnsd', x, hl_w) + hl_b[None, :, None, :]
        pad = sx == 0
        q = jnp.einsum('bnsd,neod->bneso', sx, wq)
        k = jnp.einsum('bnsd,nod->bnso', sx, wk)
        v = jnp.einsum('bnsd,nod->bnso', sx, wv)
        causal = jnp.where(jnp.tril(jnp.ones((s, s), bool)), 0.0, -jnp.inf).astype(x.dtype)
        scores = jnp.einsum('bnesd,bntd->bnest', q, k) * d ** 0.5 + causal
        att = jax.nn.softmax(scores, axis=-1)
        qkv = jnp.einsum('bnest,bntd->bnesd', att, v)
        qkv = jnp.where(pad[:, :, None], 0.0, qkv)
        out = jnp.transpose(qkv, (0, 1, 3, 2, 4)).reshape(b, nh, s, ne * d)
        gs = jax.nn.softmax(jnp.einsum('bnsf,nef->bnse', out, gate_w) + gate_b[None, :, None, :], axis=-1)
        mixed = jnp.einsum('bnsed,bnse->bnsd', out.reshape(b, nh, s, ne, d), gs)
        resid = sx[jnp.arange(nh), jnp.arange(nh)]
        hn = layernorm(mixed + resid, ln_g, ln_b)
        f_n = jnp.transpose(hn, (0, 2, 1, 3)).reshape(b, s, h)
        fx = f_n.reshape(b, s, nh, d)
        pm = fx == 0
        hx = jnp.where(pm, 0.0, fx @ fc1_w.T + fc1_b)
        hx = jax.nn.relu(hx)
        hx = jnp.where(pm, 0.0, hx @ fc2_w.T + fc2_b)
        hx = layernorm(hx + fx, fnorm_g, fnorm_b)
        fout = hx.reshape(b, s, h)
        fg = jax.nn.softmax(fout @ fgate_w.T, axis=-1)
        return (fout.reshape(b, s, nh, d) * fg[..., None]).reshape(b, s, h)

    def _L1_attn_ref(x, Wqkv, bqkv, Wproj, bproj, temperature):
        import jax, jax.numpy as jnp
        import numpy as np
        A, Bc, Cc = (0.5, 1.0, 1.0)
        H = 8
        EPS = 1e-12

        def _normalize(t):
            n = jnp.linalg.norm(t, axis=-1, keepdims=True)
            return t / jnp.maximum(n, EPS)
        B, N, C = x.shape
        D = C // H
        scale = float(D) ** 0.25
        qkv = (x @ Wqkv.T + bqkv).reshape(B, N, 3, H, D)
        qkv = jnp.transpose(qkv, (2, 0, 3, 1, 4))
        q, k, v = (qkv[0], qkv[1], qkv[2])
        q = q * scale
        v1 = jnp.concatenate([jnp.ones((B, H, N, 1), dtype=v.dtype), v], axis=-1)
        qn = _normalize(q) * (scale * temperature)
        kn = _normalize(k) * scale
        vN = v1 / N
        kv_mod = jnp.einsum('bhni,bhnj,bhne->bhije', kn, kn, vN)
        kv = jnp.einsum('bhnd,bhne->bhde', kn, vN)
        vsum = jnp.sum(vN, axis=-2)[:, :, None, :]
        y = A * jnp.einsum('bhni,bhnj,bhije->bhne', qn, qn, kv_mod) + scale ** 2 * Bc * jnp.einsum('bhnd,bhde->bhne', qn, kv) + scale ** 4 * Cc * vsum
        y_norm, y = (y[..., :1], y[..., 1:])
        y = y / y_norm
        out = jnp.transpose(y, (0, 2, 1, 3)).reshape(B, N, H * D)
        return out @ Wproj.T + bproj

    def _L1_ffn_ref(x, gamma, beta, Wr, br, W1, b1, W2, b2):
        import jax, jax.numpy as jnp
        import numpy as np
        E = 8
        K = 2
        D = 64
        H = 128
        DOUT = 64
        EPS = 1e-05
        mu = jnp.mean(x, axis=-1, keepdims=True)
        var = jnp.mean(jnp.square(x - mu), axis=-1, keepdims=True)
        xn = (x - mu) * jax.lax.rsqrt(var + EPS) * gamma + beta
        logits = jnp.einsum('bsd,de->bse', xn, Wr) + br
        top_vals, top_idx = jax.lax.top_k(logits, K)
        w = jax.nn.softmax(top_vals, axis=-1)
        w_full = jnp.einsum('bsk,bske->bse', w, jax.nn.one_hot(top_idx, E, dtype=w.dtype))
        y = jnp.zeros(x.shape[:-1] + (DOUT,), x.dtype)
        for e in range(E):
            h = jax.nn.gelu(jnp.einsum('bsd,dh->bsh', xn, W1[e]) + b1[e], approximate=False)
            y_e = jnp.einsum('bsh,hd->bsd', h, W2[e]) + b2[e]
            y = y + y_e * w_full[..., e, None]
        return y
    h = _L0_tok_ref(x, L0_tok_w, L0_tok_b, L0_tok_gamma, L0_tok_beta, L0_tok_alpha)
    h = h + _L0_attn_ref(_layernorm(h, axis=-1), L0_attn_Wq, L0_attn_Wk, L0_attn_Wv, L0_attn_Wo, L0_attn_bo)
    h = h + _L0_ffn_ref(_layernorm(h, axis=-1), L0_ffn_hl_w, L0_ffn_hl_b, L0_ffn_wq, L0_ffn_wk, L0_ffn_wv, L0_ffn_gate_w, L0_ffn_gate_b, L0_ffn_ln_g, L0_ffn_ln_b, L0_ffn_fc1_w, L0_ffn_fc1_b, L0_ffn_fc2_w, L0_ffn_fc2_b, L0_ffn_fnorm_g, L0_ffn_fnorm_b, L0_ffn_fgate_w)
    h = h + _L1_attn_ref(_layernorm(h, axis=-1), L1_attn_Wqkv, L1_attn_bqkv, L1_attn_Wproj, L1_attn_bproj, L1_attn_temperature)
    h = h + _L1_ffn_ref(_layernorm(h, axis=-1), L1_ffn_gamma, L1_ffn_beta, L1_ffn_Wr, L1_ffn_br, L1_ffn_W1, L1_ffn_b1, L1_ffn_W2, L1_ffn_b2)
    return h

_drawn_inputs = setup_inputs


def setup_inputs(seed=0):
    import zlib

    import numpy as np

    out = dict(_drawn_inputs(seed))
    spreads = {'L0_tok_gamma': (1.0, 0.2),
     'L0_tok_beta': (0.0, 0.1),
     'L0_ffn_ln_g': (1.0, 0.2),
     'L0_ffn_ln_b': (0.0, 0.357),
     'L0_ffn_fnorm_g': (1.0, 0.2),
     'L0_ffn_fnorm_b': (0.0, 0.346),
     'L1_attn_bqkv': (0.0, 0.51),
     'L1_attn_bproj': (0.0, 0.1),
     'L1_attn_temperature': (1.0, 0.6),
     'L1_ffn_br': (0.0, 0.516)}
    factors = {'L0_attn_bo': 5.482,
     'L0_ffn_wq': 8.0,
     'L0_ffn_wk': 8.0,
     'L0_ffn_gate_w': 8.0,
     'L0_ffn_gate_b': 8.0,
     'L0_ffn_fc1_w': 8.0,
     'L0_ffn_fc1_b': 8.0,
     'L0_ffn_fc2_w': 6.6,
     'L0_ffn_fc2_b': 3.298,
     'L1_attn_Wqkv': 7.563,
     'L1_attn_Wproj': 3.1,
     'L1_ffn_gamma': 8.0,
     'L1_ffn_beta': 8.0,
     'L1_ffn_Wr': 4.289,
     'L1_ffn_W1': 4.886,
     'L1_ffn_b1': 8.0,
     'L1_ffn_W2': 4.795,
     'L1_ffn_b2': 14.736}
    for name, (base, spread) in spreads.items():
        noise = np.random.default_rng([zlib.crc32(name.encode()), seed]).standard_normal(out[name].shape)
        drawn = base * np.exp(spread * noise) if base else spread * noise
        out[name] = jnp.asarray(drawn.astype(out[name].dtype))
    for name, factor in factors.items():
        out[name] = (out[name] * factor).astype(out[name].dtype)
    return out
```

```python
from contextlib import ExitStack

import numpy as np
import concourse.bass as bass
from concourse import mybir

F32 = mybir.dt.float32
BF16 = mybir.dt.bfloat16
U32 = mybir.dt.uint32
ALU = mybir.AluOpType
ACT = mybir.ActivationFunctionType
AX = mybir.AxisListType

B, T_IN, C = 32, 375, 64
TAPS, STRIDE = 5, 2
N = (T_IN + STRIDE - 1) // STRIDE
PAD = ((N - 1) * STRIDE + TAPS - T_IN) // 2
P = N // 2
HALVES = 2
TILES = B * HALVES
TOK_EPS = 1e-3
LN_EPS = 1e-5
LN2_EPS = 1e-8

HEADS, HEAD = 8, 32
NH, NE, D = 4, 4, 16
TH, TD = 8, 8
E, HID = 8, 128
QUAD = 4
MASKED = -1.0e30
TS = float(TD) ** 0.25
TS2, TS4 = TS * TS, TS ** 4


WEIGHTS = {}


def _place(name, cols):
    start = WEIGHTS["_"] if "_" in WEIGHTS else 0
    WEIGHTS[name] = (start, cols)
    WEIGHTS["_"] = start + cols


for _name, _cols in [
    ("conv", TAPS * C), ("conv_b", C), ("tok_gamma", C), ("tok_beta", C), ("tok_alpha", C),
    ("wq", 256), ("wk", 256), ("wv", 256), ("wo", 2 * C), ("bo", C),
    ("hl_t", 128), ("hl_bt", 1), ("hl", C), ("hl_b", C), ("ewq", NE * 128), ("ewk", 128), ("ewv", C),
    ("pick", NE * 84), ("gate_b", 16), ("ln_g", C), ("ln_b", C), ("fc1", 128), ("fc1_b", 1),
    ("fc2", C), ("fc2_b", C), ("fn_g", C), ("fn_b", C), ("fgate", NH * C),
    ("wqkv", 192), ("bqkv", 192), ("wproj", C), ("bproj", C), ("temp", TH),
    ("gamma", C), ("beta", C), ("br", E), ("w1", E * HID), ("wr", E), ("b1", E), ("w2", E * C),
    ("b2", C),
]:
    _place(_name, _cols)
W_COLS = WEIGHTS.pop("_")


def build(nc, x_pad, weights, out):
    with ExitStack() as ctx:
        def sb(name, shape, dt=F32):
            return ctx.enter_context(nc.sbuf_tensor(name, shape, dt))

        stream = sb("stream", [P, TILES, C])
        wsb = sb("wsb", [128, W_COLS])
        ident = sb("ident", [128, 128])
        identb = sb("identb", [P, P], BF16)
        ones = sb("ones", [P, 128])
        neg_half = sb("neg_half", [P, 64])

        residual = sb("residual", [P, HALVES, C])
        w_parts = sb("w_parts", [128, 3, E * (HID + 1)], BF16)

        def w(name, rows=128):
            a, n = WEIGHTS[name]
            return wsb[0:rows, a:a + n]

        env = dict(nc=nc, stream=stream, w=w, ident=ident, identb=identb, ones=ones,
                   neg_half=neg_half, residual=residual, w_parts=w_parts)
        tokenizer(env, x_pad, weights, wsb)
        alibi_attention(env)
        expert_attention(env)
        taylor_attention(env)
        mixture(env)
        write_out(env, out)


def clear_semaphores(nc, sems):
    with nc.Block() as block:
        @block.sync
        def _(sp):
            for s in sems:
                sp.sem_clear(s)


def tokenizer(env, x_pad, weights, wsb):
    nc, stream, w, w_parts = env["nc"], env["stream"], env["w"], env["w_parts"]
    ident, identb, ones, neg_half = env["ident"], env["identb"], env["ones"], env["neg_half"]
    CH = 4
    CT = CH * HALVES
    CHUNKS = B // CH
    COUNT = float(N * C)
    WIN = TAPS * C
    with ExitStack() as ctx:
        def sb(name, shape, dt=F32):
            return ctx.enter_context(nc.sbuf_tensor(name, shape, dt))

        sems = []

        def sem(name):
            sems.append(ctx.enter_context(nc.semaphore(name)))
            return sems[-1]

        window = [sb(f"window{i}", [P, CT, WIN]) for i in range(2)]
        prod = [sb(f"prod{i}", [P, CT, C]) for i in range(TAPS)]
        square = sb("tok_square", [P, CT, C])
        sums = sb("tok_sums", [P, CT])
        mean = sb("tok_mean", [P, CH])
        var = sb("tok_var", [P, CH])
        rest = sb("tok_rest", [128, E * (HID + 1)])
        rstd = sb("tok_rstd", [P, CH])
        ps = ctx.enter_context(nc.psum_tensor("tok_ps", [128, 512], F32))
        weights_in = sem("weights_in")
        window_in = [sem("window_in0"), sem("window_in1")]
        window_used = sem("window_used")
        const_set = sem("const_set")
        tok_dve = sem("tok_dve")
        tok_squared = sem("tok_squared")
        tok_rstd_set = sem("tok_rstd_set")
        parts_set = sem("parts_set")
        sums_ready = sem("sums_ready")
        totals_ready = sem("totals_ready")
        ctx.callback(clear_semaphores, nc, sems)
        block = ctx.enter_context(nc.Block())

        def windows(c, h):
            row = (T_IN + 2 * PAD) * C
            return bass.AP(tensor=x_pad.tensor, offset=c * CH * row + h * P * STRIDE * C,
                           ap=[[STRIDE * C, P], [row, CH], [1, WIN]])

        @block.sync
        def _(sp):
            sp.dma_start(wsb[:], weights).then_inc(weights_in, 16)
            for c in range(CHUNKS):
                if c >= 2:
                    sp.wait_ge(window_used, c - 1)
                for h in range(HALVES):
                    sp.dma_start(window[c % 2][:, h:CT:HALVES, :], windows(c, h)).then_inc(window_in[c % 2], 16)

        @block.gpsimd
        def _(pool):
            nc.gpsimd.memset(ones[:], 1.0).then_inc(const_set, 1)
            nc.gpsimd.memset(neg_half[:], -0.5).then_inc(const_set, 1)
            nc.gpsimd.memset(ident[:], 0.0).then_inc(const_set, 1)
            nc.gpsimd.memset(identb[:], 0.0).then_inc(const_set, 1)
            pool.wait_ge(const_set, 4)
            for m, n in ((ident, 128), (identb, P)):
                nc.gpsimd.affine_select(out=m[:], in_=m[:], compare_op=ALU.not_equal, fill=1.0, base=0,
                                        pattern=[[-1, n]], channel_multiplier=1).then_inc(const_set, 1)
            pool.wait_ge(weights_in, 16)
            start, _ = WEIGHTS["w1"]
            whole = wsb[:, start:start + E * (HID + 1)]
            for c in range(CHUNKS):
                pool.wait_ge(tok_squared, 2 * c + 1)
                nc.gpsimd.tensor_tensor(rstd[:], var[:], neg_half[:, 0:CH], ALU.pow).then_inc(tok_rstd_set, 1)
                if c == 0:
                    nc.gpsimd.tensor_copy(w_parts[:, 0], whole).then_inc(parts_set, 1)
                if c == 1:
                    pool.wait_ge(parts_set, 1)
                    nc.gpsimd.tensor_tensor(rest[:], whole, w_parts[:, 0], ALU.subtract).then_inc(parts_set, 1)
                if c == 2:
                    pool.wait_ge(parts_set, 2)
                    nc.gpsimd.tensor_copy(w_parts[:, 1], rest[:]).then_inc(parts_set, 1)
                if c == 3:
                    nc.gpsimd.tensor_copy(w_parts[:, 2], w_parts[:, 0]).then_inc(parts_set, 1)
                if c == 4:
                    pool.wait_ge(parts_set, 4)
                    nc.gpsimd.tensor_tensor(w_parts[0:C, 2], rest[0:C], w_parts[0:C, 1], ALU.subtract)\
                        .then_inc(parts_set, 1)

        @block.tensor
        def _(pe):
            pe.wait_ge(const_set, 2)
            for c in range(2 * CHUNKS):
                pe.wait_ge(sums_ready, c + 1)
                nc.tensor.matmul(ps[0:P, 0:CT], ones[:, 0:P], sums[:], start=True, stop=True)\
                    .then_inc(totals_ready, 1)

        @block.vector
        def _(dve):
            step = [0]

            def link(ins):
                step[0] += 1
                ins.then_inc(tok_dve, 1)
                dve.wait_ge(tok_dve, step[0])

            def over_tiles(name):
                return w(name, P).unsqueeze(1).broadcast_to([P, CT, C])

            def by_row(t):
                return t[:].unsqueeze(2).broadcast_to([P, CH, HALVES * C])

            def rows(t):
                return t.rearrange("p (b h) c -> p b (h c)", h=HALVES)

            dve.wait_ge(weights_in, 16)
            for c in range(CHUNKS):
                y = stream[:, c * CT:(c + 1) * CT, :]
                dve.wait_ge(window_in[c % 2], 32 * (c // 2 + 1))
                for k in range(TAPS):
                    taps = w("conv", P)[:, k * C:(k + 1) * C].unsqueeze(1).broadcast_to([P, CT, C])
                    ins = nc.vector.tensor_tensor(prod[k][:], window[c % 2][:, :, k * C:(k + 1) * C], taps,
                                                  ALU.mult)
                    if k < TAPS - 1:
                        ins.then_inc(tok_dve, 1)
                        step[0] += 1
                    else:
                        ins.then_inc(window_used, 1)
                dve.wait_ge(window_used, c + 1)
                dve.wait_ge(tok_dve, step[0])
                link(nc.vector.tensor_tensor(prod[0][:], prod[0][:], prod[1][:], ALU.add))
                link(nc.vector.tensor_tensor(prod[2][:], prod[2][:], prod[3][:], ALU.add))
                link(nc.vector.tensor_tensor(prod[0][:], prod[0][:], prod[2][:], ALU.add))
                link(nc.vector.tensor_tensor(prod[4][:], prod[4][:], over_tiles("conv_b"), ALU.add))
                link(nc.vector.tensor_tensor(y, prod[0][:], prod[4][:], ALU.add))
                nc.vector.tensor_reduce(sums[:], y, AX.X, ALU.add).then_inc(sums_ready, 1)
                dve.wait_ge(totals_ready, 2 * c + 1)
                totals = ps[0:P, 0:CT].rearrange("p (b h) -> p b h", h=HALVES)
                link(nc.vector.tensor_reduce(mean[:], totals, AX.X, ALU.add))
                link(nc.vector.tensor_scalar(mean[:], mean[:], 1.0 / COUNT, None, ALU.mult))
                link(nc.vector.tensor_tensor(rows(y), rows(y), by_row(mean), ALU.subtract))
                link(nc.vector.tensor_tensor(square[:], y, y, ALU.mult))
                nc.vector.tensor_reduce(sums[:], square[:], AX.X, ALU.add).then_inc(sums_ready, 1)
                dve.wait_ge(totals_ready, 2 * c + 2)
                nc.vector.tensor_reduce(var[:], totals, AX.X, ALU.add).then_inc(tok_dve, 1)
                step[0] += 1
                dve.wait_ge(tok_dve, step[0])
                nc.vector.tensor_scalar(var[:], var[:], 1.0 / COUNT, TOK_EPS, ALU.mult, ALU.add)\
                    .then_inc(tok_squared, 2)
                dve.wait_ge(tok_rstd_set, c + 1)
                link(nc.vector.tensor_tensor(rows(y), rows(y), by_row(rstd), ALU.mult))
                link(nc.vector.tensor_tensor(y, y, over_tiles("tok_gamma"), ALU.mult))
                link(nc.vector.tensor_tensor(y, y, over_tiles("tok_beta"), ALU.add))
                link(nc.vector.tensor_scalar(square[:], y, 0.0, None, ALU.min))
                link(nc.vector.tensor_tensor(square[:], square[:], over_tiles("tok_alpha"), ALU.mult))
                link(nc.vector.scalar_tensor_tensor(y, y, 0.0, square[:], ALU.max, ALU.add))


class Steps:

    def __init__(self, eng, sem):
        self.eng, self.sem, self.base, self.n = eng, sem, 0, 0

    def mark(self, ins):
        self.n += 1
        ins.then_inc(self.sem, 1)

    def settle(self):
        self.eng.wait_ge(self.sem, self.base + self.n)

    def link(self, ins):
        self.mark(ins)
        self.settle()

    def loop(self, i, per_turn):
        self.start, self.per_turn = self.base + self.n, per_turn
        self.base, self.n = self.start + i * per_turn, 0

    def end(self, turns):
        assert self.n == self.per_turn, self.n
        self.base, self.n = self.start + turns * self.per_turn, 0


def need(eng, sem, value):
    if not (isinstance(value, int) and value <= 0):
        eng.wait_ge(sem, value)


def row_loop(eng, body, steps=None, per_turn=0, ahead=1):
    body(0, 0, True, False)
    turns = (B - 2) // 2
    with eng.Fori(0, turns) as i:
        if steps:
            steps.loop(i, per_turn)
        body(i * 2 + 1, 1, False, False)
        body(i * 2 + 2, 0, False, False)
    if steps:
        steps.end(turns)
    body(B - 1, 1, False, True)


def alibi_attention(env):
    nc, stream, w = env["nc"], env["stream"], env["w"]
    ident, identb, ones, neg_half = env["ident"], env["identb"], env["ones"], env["neg_half"]
    U = HEADS // QUAD
    SLOPES = [0.5 ** (h + 1) for h in range(HEADS)]
    with ExitStack() as ctx:
        def sb(name, shape, dt=F32):
            return ctx.enter_context(nc.sbuf_tensor("al_" + name, shape, dt))

        def psum(name, shape, dt=F32):
            return ctx.enter_context(nc.psum_tensor("al_" + name, shape, dt))

        def sem(name):
            return ctx.enter_context(nc.semaphore("al_" + name))

        rel = sb("rel", [P, N])
        biasA = sb("biasA", [P, HEADS, P], BF16)
        biasB = sb("biasB", [P, HEADS, N], BF16)
        quad_mask = sb("quad_mask", [128, QUAD])
        stats = sb("stats", [P, HALVES, 6])
        moments = sb("moments", [P, HALVES, 2])
        variance = sb("variance", [P, HALVES])
        rstd = sb("rstd", [P, HALVES])
        eps = sb("eps", [P, HALVES])
        xn = sb("xn", [P, HALVES, C])
        xT = sb("xT", [C, N])
        qT = [sb(f"qT{i}", [128, U, N]) for i in range(2)]
        kT = sb("kT", [128, U, N])
        kpad = [sb(f"kpad{i}", [128, QUAD, U, N]) for i in range(2)]
        v = [sb(f"v{i}", [P, HALVES, HEADS * HEAD]) for i in range(2)]
        negmax = [sb(f"negmax{i}", [P, 2 * QUAD]) for i in range(2)]
        prob = [sb(f"prob{i}", [P, 3, 2 * N]) for i in range(2)]
        probT = [sb(f"probT{i}", [P, 3, 2 * N]) for i in range(2)]
        rec = sb("rec", [128, N])
        onT = sb("onT", [128, U, N])
        added = sb("added", [P, HALVES, C])

        S = psum("S", [128, 3, 512])
        PT = psum("PT", [128, 3, 512])
        O = psum("O", [128, 512])
        X = psum("X", [128, 512])

        rel_set, bias_set, masks_set = sem("rel_set"), sem("bias_set"), sem("masks_set")
        stats_ready, rstd_ready, xn_ready = sem("stats_ready"), sem("rstd_ready"), sem("xn_ready")
        var_set, stats_settled = sem("var_set"), sem("stats_settled")
        misc_full, misc_free = sem("misc_full"), sem("misc_free")
        kT_ready, kpad_ready = sem("kT_ready"), sem("kpad_ready")
        s_full, s_free, max_done = sem("s_full"), sem("s_free"), sem("max_done")
        pt_full, pt_act, pt_dve = sem("pt_full"), sem("pt_act"), sem("pt_dve")
        o_full, o_free = sem("o_full"), sem("o_free")
        onT_ready = sem("onT_ready")
        dve_step = sem("dve_step")
        block = ctx.enter_context(nc.Block())

        def fill(b, what):
            if isinstance(b, int) and b == 0:
                return {"xT": 4, "k": 5, "q": 6, "v": 7}[what]
            if isinstance(b, int) and b == B - 1:
                return 8 + 5 * (b - 1) + {"out": 0, "tail": 1}[what]
            return b * 5 + 3 + {"xT": 0, "k": 1, "q": 2, "out": 3, "v": 4}[what]

        @block.tensor
        def _(pe):
            def fill_X(n, matmuls):
                need(pe, misc_free, n)
                for k, (dst, a, m, kw) in enumerate(matmuls):
                    last = nc.tensor.matmul(dst, a, m, **kw)
                last.then_inc(misc_full, 1)

            def transposed_x(n, row):
                pe.wait_ge(xn_ready, row + 1)
                fill_X(n, [(X[0:C, h * P:(h + 1) * P], xn[:, h, :], ident[0:P, 0:P], dict(start=True, stop=True))
                           for h in range(HALVES)])

            def project_qk(n, name):
                need(pe, misc_free, n)
                for g in range(U):
                    last = nc.tensor.matmul(X[:, g * N:(g + 1) * N], w(name, C)[:, g * 128:(g + 1) * 128], xT[:],
                                            start=True, stop=True)
                last.then_inc(misc_full, 1)

            def project_v(n):
                need(pe, misc_free, n)
                for h in range(HALVES):
                    last = nc.tensor.matmul(X[0:P, h * 256:(h + 1) * 256], xT[:, h * P:(h + 1) * P], w("wv", C),
                                            start=True, stop=True)
                last.then_inc(misc_full, 1)

            def scores(b, par, g):
                u = b * U + g
                if g == 0:
                    pe.wait_ge(kpad_ready, b + 1)
                for k in range(3):
                    need(pe, s_free, 3 * u - 2 + k)
                    if k == 0:
                        q, s, bias = qT[par][:, g, 0:P], kpad[par][:, :, g, 0:P], biasA[:, QUAD * g:QUAD * g + QUAD, :]
                    else:
                        j = 2 * (k - 1)
                        q, s, bias = qT[par][:, g, P:N], kpad[par][:, j:j + 2, g, :], biasB[:, QUAD * g + j:QUAD * g + j + 2, :]
                    nc.tensor.matmul(S[0:P, k, 0:2 * N], q, s, start=True, stop=False)
                    nc.tensor.matmul(S[0:P, k, 0:2 * N], identb[:], bias, start=False, stop=True).then_inc(s_full, 1)

            def transpose_probs(b, par, g):
                u = b * U + g
                need(pe, s_free, 3 * u + 3)
                need(pe, pt_act, u)
                need(pe, pt_dve, u)
                p = prob[g % 2]
                for k in range(3):
                    for j in (range(2 * k, 2 * k + 2) if k < 2 else range(QUAD)):
                        lo = p[:, 1 + j // 2, (j % 2) * N:(j % 2) * N + P]
                        hi = p[:, 1 + j // 2, (j % 2) * N + P:(j % 2) * N + N]
                        if k < 2:
                            nc.tensor.transpose(PT[0:P, k, (j % 2) * N:(j % 2) * N + P], p[:, 0, j * P:(j + 1) * P],
                                                ident[0:P, 0:P])
                            last = nc.tensor.transpose(PT[0:P, k, (j % 2) * N + P:(j % 2) * N + N], lo, ident[0:P, 0:P])
                        else:
                            last = nc.tensor.transpose(PT[0:P, 2, j * P:(j + 1) * P], hi, ident[0:P, 0:P])
                    last.then_inc(pt_full, 1)

            def weigh_values(b, par, g):
                u = b * U + g
                pe.wait_ge(pt_act, u + 1)
                pe.wait_ge(pt_dve, u + 1)
                need(pe, o_free, u)
                pT = probT[g % 2]
                for c in range(2):
                    for s in range(HALVES):
                        for j in range(QUAD):
                            h = QUAD * g + j
                            val = (v[par][:, s, h * HEAD:(h + 1) * HEAD], ones[:, 0:HEAD])[c]
                            if s == 0:
                                dst = O[32 * j:32 * j + 32, c * N:(c + 1) * N]
                                src = pT[:, j // 2, (j % 2) * N:(j % 2) * N + N]
                            else:
                                dst = O[32 * j:32 * j + 32, c * N + P:(c + 1) * N]
                                src = pT[:, 2, j * P:(j + 1) * P]
                            last = nc.tensor.matmul(dst, val, src, start=(s == 0), stop=(s == 1),
                                                    tile_position=(0, 32 * j), skip_group_check=True)
                last.then_inc(o_full, 1)

            def project_out(n, row):
                pe.wait_ge(onT_ready, (row + 1) * U)
                need(pe, misc_free, n)
                for h in range(HALVES):
                    for g in range(U):
                        last = nc.tensor.matmul(X[0:P, h * C:(h + 1) * C], onT[:, g, h * P:(h + 1) * P],
                                                w("wo")[:, g * C:(g + 1) * C], start=(g == 0), stop=(g == U - 1))
                last.then_inc(misc_full, 1)

            def body(b, par, first, last):
                scores(b, par, 1)
                if not last:
                    transposed_x(fill(b, "xT"), b + 1)
                transpose_probs(b, par, 0)
                if not first:
                    weigh_values(b - 1, 1 - par, 1)
                if not last:
                    pe.wait_ge(misc_free, fill(b, "xT") + 1)
                    project_qk(fill(b, "k"), "wk")
                    project_qk(fill(b, "q"), "wq")
                if not first:
                    project_out(fill(b, "out"), b - 1)
                if not last:
                    pe.wait_ge(misc_free, fill(b, "q") + 1)
                    scores(b + 1, 1 - par, 0)
                transpose_probs(b, par, 1)
                weigh_values(b, par, 0)
                if not last:
                    project_v(fill(b, "v"))
                else:
                    weigh_values(b, par, 1)
                    project_out(fill(b, "tail"), b)

            pe.wait_ge(bias_set, 2 * HEADS)
            transposed_x(0, 0)
            pe.wait_ge(misc_free, 1)
            project_qk(1, "wk")
            project_qk(2, "wq")
            project_v(3)
            scores(0, 0, 0)
            row_loop(pe, body)

        @block.scalar
        def _(act):
            def copy_out(n, dst, rows, cols, scale=1.0):
                act.wait_ge(misc_full, n + 1)
                nc.scalar.activation(dst, X[0:rows, 0:cols], ACT.Copy, scale=scale).then_inc(misc_free, 1)

            def flat(t):
                return t.rearrange("p a b -> p (a b)")

            def exps(b, g):
                u = b * U + g
                p = prob[g % 2]
                for k in range(3):
                    act.wait_ge(max_done, 3 * u + k + 1)
                    for j in (range(QUAD) if k == 0 else range(2 * k - 2, 2 * k)):
                        cols = slice(j * P, (j + 1) * P) if k == 0 else slice((j % 2) * N, (j % 2) * N + N)
                        m = j if k == 0 else QUAD + j
                        last = nc.scalar.activation(p[:, k, cols], S[0:P, k, cols], ACT.Exp,
                                                    bias=negmax[g % 2][:, m:m + 1])
                    last.then_inc(s_free, 1)

            def copy_probs(b, g):
                act.wait_ge(pt_full, 3 * (b * U + g) + 1)
                nc.scalar.activation(probT[g % 2][:, 0, :], PT[0:P, 0, 0:2 * N], ACT.Copy).then_inc(pt_act, 1)

            def keys(n, b):
                need(act, kpad_ready, b)
                act.wait_ge(misc_full, n + 1)
                nc.scalar.activation(flat(kT[:]), X[:, 0:U * N], ACT.Copy).then_inc(misc_free, 1)
                act.wait_ge(misc_free, n + 1)
                act.sem_inc(kT_ready, 1)

            def body(b, par, first, last):
                exps(b, 1)
                if not last:
                    copy_out(fill(b, "xT"), xT[:], C, N)
                copy_probs(b, 0)
                if not last:
                    keys(fill(b, "k"), b + 1)
                    copy_out(fill(b, "q"), flat(qT[1 - par][:]), 128, U * N, HEAD ** -0.5)
                    exps(b + 1, 0)
                copy_probs(b, 1)
                if not last:
                    copy_out(fill(b, "v"), flat(v[1 - par][:]), P, 512)

            copy_out(0, xT[:], C, N)
            keys(1, 0)
            copy_out(2, flat(qT[0][:]), 128, U * N, HEAD ** -0.5)
            copy_out(3, flat(v[0][:]), P, 512)
            exps(0, 0)
            row_loop(act, body)

        @block.gpsimd
        def _(pool):
            nc.gpsimd.memset(eps[:], LN_EPS).then_inc(var_set, 1)
            nc.gpsimd.memset(quad_mask[:], 1.0).then_inc(masks_set, 1)
            pool.wait_ge(masks_set, 1)
            nc.gpsimd.affine_select(out=quad_mask[:], in_=quad_mask[:], compare_op=ALU.is_ge, fill=0.0, base=0,
                                    pattern=[[-32, QUAD]], channel_multiplier=1).then_inc(masks_set, 1)
            pool.wait_ge(masks_set, 2)
            nc.gpsimd.affine_select(out=quad_mask[:], in_=quad_mask[:], compare_op=ALU.is_ge, fill=0.0, base=31,
                                    pattern=[[32, QUAD]], channel_multiplier=-1).then_inc(masks_set, 1)
            pool.wait_ge(masks_set, 3)
            nc.gpsimd.iota(rel[:], pattern=[[1, N]], base=0, channel_multiplier=-1,
                           allow_small_or_imprecise_dtypes=True).then_inc(rel_set, 1)
            pool.wait_ge(rel_set, 1)
            for h in range(HEADS):
                nc.gpsimd.tensor_scalar(biasA[:, h, :], rel[:, 0:P], SLOPES[h], None, ALU.mult).then_inc(rel_set, 1)
                nc.gpsimd.tensor_scalar(biasB[:, h, :], rel[:], -float(P), SLOPES[h], ALU.add, ALU.mult)\
                    .then_inc(rel_set, 1)
            pool.wait_ge(rel_set, 1 + 2 * HEADS)
            for h in range(HEADS):
                for t, cols, shift in ((biasA, P, 0), (biasB, N, P)):
                    nc.gpsimd.affine_select(out=t[:, h, :], in_=t[:, h, :], compare_op=ALU.is_ge, fill=MASKED,
                                            base=shift, pattern=[[-1, cols]], channel_multiplier=1)\
                        .then_inc(bias_set, 1)

            def rstds(b):
                pool.wait_ge(stats_ready, b + 1)
                nc.gpsimd.tensor_tensor(variance[:], moments[:, :, 1], eps[:], ALU.add).then_inc(var_set, 1)
                pool.wait_ge(var_set, b + 2)
                nc.gpsimd.tensor_tensor(rstd[:], variance[:], neg_half[:, 0:HALVES], ALU.pow).then_inc(rstd_ready, 1)

            def mask_keys(b, par):
                pool.wait_ge(kT_ready, b + 1)
                nc.gpsimd.tensor_tensor(kpad[par][:].rearrange("p j g n -> p j (g n)"),
                                        kT[:].rearrange("p g n -> p (g n)").unsqueeze(1).broadcast_to([128, QUAD, U * N]),
                                        quad_mask[:].unsqueeze(2).broadcast_to([128, QUAD, U * N]), ALU.mult)\
                    .then_inc(kpad_ready, 1)

            def body(b, par, first, last):
                if not last:
                    rstds(b + 1)
                    mask_keys(b + 1, 1 - par)

            rstds(0)
            mask_keys(0, 0)
            row_loop(pool, body)

        @block.vector
        def _(dve):
            steps = Steps(dve, dve_step)
            PER_ROW = 8

            def statistics(b):
                for h in range(HALVES):
                    steps.mark(nc.vector.bn_stats(stats[:, h, :], stream[:, b * HALVES + h, :]))
                steps.settle()
                dve.sem_inc(stats_settled, 1)
                nc.vector.bn_aggr(moments[:, 0, :], stats[:, 0, :])
                last = nc.vector.bn_aggr(moments[:, 1, :], stats[:, 1, :])
                last.then_inc(stats_ready, 1)

            def normalise(b):
                dve.wait_ge(stats_ready, b + 1)
                dve.wait_ge(rstd_ready, b + 1)
                for h in range(HALVES):
                    last = nc.vector.tensor_scalar(xn[:, h, :], stream[:, b * HALVES + h, :], moments[:, h, 0:1],
                                                   rstd[:, h:h + 1], ALU.subtract, ALU.mult)
                last.then_inc(xn_ready, 1)

            def maxima(b, g):
                u = b * U + g
                m = negmax[g % 2]
                for k in range(3):
                    dve.wait_ge(s_full, 3 * u + k + 1)
                    if k == 0:
                        src, dst = S[0:P, 0, 0:2 * N].rearrange("p (j s) -> p j s", j=QUAD), m[:, 0:QUAD]
                    else:
                        src = S[0:P, k, 0:2 * N].rearrange("p (j s) -> p j s", j=2)
                        dst = m[:, QUAD + 2 * k - 2:QUAD + 2 * k]
                    nc.vector.tensor_reduce(dst, src, AX.X, ALU.max, negate=True).then_inc(max_done, 1)

            def copy_probs(b, g):
                dve.wait_ge(pt_full, 3 * (b * U + g) + 3)
                nc.vector.tensor_copy(probT[g % 2][:, 1:3, :], PT[0:P, 1:3, 0:2 * N]).then_inc(pt_dve, 1)

            def divide(b, g):
                dve.wait_ge(o_full, b * U + g + 1)
                steps.link(nc.vector.reciprocal(rec[:], O[:, N:2 * N]))
                steps.link(nc.vector.tensor_tensor(onT[:, g, :], O[:, 0:N], rec[:], ALU.mult))
                dve.sem_inc(o_free, 1)
                dve.sem_inc(onT_ready, 1)

            def add_out(n, b):
                dve.wait_ge(misc_full, n + 1)
                bo = w("bo", P).unsqueeze(1).broadcast_to([P, HALVES, C])
                steps.link(nc.vector.tensor_tensor(added[:], X[0:P, 0:HALVES * C].rearrange("p (h c) -> p h c", h=HALVES), bo,
                                                   ALU.add))
                dve.sem_inc(misc_free, 1)
                y = stream[:, bass.ds(b * HALVES, HALVES), :]
                steps.link(nc.vector.tensor_tensor(y, y, added[:], ALU.add))

            def body(b, par, first, last):
                if not last:
                    statistics(b + 1)
                maxima(b, 1)
                if not last:
                    normalise(b + 1)
                copy_probs(b, 0)
                if not first:
                    divide(b - 1, 1)
                    add_out(fill(b, "out"), b - 1)
                if not last:
                    maxima(b + 1, 0)
                copy_probs(b, 1)
                divide(b, 0)
                if last:
                    divide(b, 1)
                    add_out(fill(b, "tail"), b)

            statistics(0)
            normalise(0)
            maxima(0, 0)
            row_loop(dve, body, steps, 2 * PER_ROW)


def expert_attention(env):
    nc, stream, w = env["nc"], env["stream"], env["w"]
    ident, identb, neg_half = env["ident"], env["identb"], env["neg_half"]
    residual = env["residual"]
    residual_rows(env, residual)
    STEPS = 35
    K0, K1 = 128, N - 128
    PICK = 84
    with ExitStack() as ctx:
        def sb(name, shape, dt=F32):
            return ctx.enter_context(nc.sbuf_tensor("ex_" + name, shape, dt))

        def two(name, shape, dt=F32):
            return [sb(f"{name}{i}", shape, dt) for i in range(2)]

        def psum(name, shape):
            return ctx.enter_context(nc.psum_tensor("ex_" + name, shape, F32))

        quad_mask = sb("quad_mask", [128, NH])
        one_row = sb("one_row", [128, 1])
        maskA = sb("maskA", [P, NH, P], BF16)
        eps = sb("eps", [P, HALVES])
        fout = sb("fout", [P, HALVES, C])
        v9 = sb("v9", [P, HALVES * NH])
        r9 = sb("r9", [P, HALVES * NH])
        stats = sb("stats", [P, HALVES, 6])
        moments = sb("moments", [P, HALVES, 2])
        variance = sb("variance", [P, HALVES])
        rstd = sb("rstd", [P, HALVES])
        xn = sb("xn", [P, HALVES, C])
        xT = sb("xT", [C, N])
        sxT = two("sxT", [128, N])
        kT = sb("kT", [128, N])
        kpad = two("kpad", [128, NH, N])
        kpadb = two("kpadb", [128, NH, N], BF16)
        qT = two("qT", [128, NE, N])
        qTb = two("qTb", [128, NE, N], BF16)
        vals = two("vals", [128, 2, NH, 32])
        negmax = two("negmax", [P, HALVES, 128], BF16)
        qm = two("qm", [128, N])
        pT = two("pT", [128, 3, 2 * N])
        oT = two("oT", [128, NE, N])
        rec = sb("rec", [P, HALVES, NE, NH])
        glog = sb("glog", [P, HALVES, NE, NH, NE])
        outs = sb("outs", [P, HALVES, NE, NH, D])
        gate = sb("gate", [P, HALVES, NH, NE])
        top = sb("top", [P, HALVES * NH])
        gate_exp = sb("gate_exp", [P, HALVES, NH, NE])
        mixed = sb("mixed", [P, HALVES, NE, NH, D])
        fx = two("fx", [P, HALVES, C])
        cent = sb("cent", [P, HALVES, C])
        sq = sb("sq", [P, HALVES, C])
        s8 = sb("s8", [P, HALVES * NH])
        v8 = sb("v8", [P, HALVES * NH])
        r8 = sb("r8", [P, HALVES * NH])
        fxT = sb("fxT", [C, N])
        h1T = sb("h1T", [C, N])
        h1m = sb("h1m", [C, N])
        hx = sb("hx", [P, HALVES, C])
        fprod = sb("fprod", [P, HALVES, NH, C])
        fgate = sb("fgate", [P, HALVES, NH])
        fexp = sb("fexp", [P, HALVES, NH])

        R = psum("R", [128, 3, 512])
        T = psum("T", [128, 3, 512])
        O = psum("O", [128, 512])
        X = psum("X", [128, 512])

        names = """consts stats_set settled aggregate stats_ready var_set rstd_ready xn_ready kT_ready kpad_ready xT_full xT_used
            sx_full sx_used k_full q01_full q01_used q23_full q23_used v_full v_used m_full m_used pickA_full
            pickA_used pickB_full pickB_used fxT_full fxT_used fc1_full fc1_used fc2_full fc2_used r_full r_used
            t_full t_used causal_done o_full o_used gate_ready gexp_ready gs_ready mixed_ready v8_ready r8_ready
            fx_ready h1m_ready v9_ready r9_ready fout_ready fprod_ready fgate_ready fexp_ready dve_step""".split()
        sem = {n: ctx.enter_context(nc.semaphore("ex_" + n)) for n in names}
        CONSTS = 17
        DEPTH = 6
        block = ctx.enter_context(nc.Block())

        def valid(r):
            return not isinstance(r, int) or 0 <= r < B

        def row_halves(r):
            return stream[:, bass.ds(r * HALVES, HALVES), :]

        def over_halves(name):
            return w(name, P).unsqueeze(1).broadcast_to([P, HALVES, w(name, P).shape[1]])

        def heads(t):
            return t[:].rearrange("p h (n d) -> p (h n) d", n=NH)

        LN, FRONT, UNIT, TAIL, MLP, FIN, LAST = range(7)
        FILLS = [("xT", FRONT), ("m1", UNIT), ("sx", FRONT), ("m2", UNIT), ("pickA", TAIL), ("fc2", FIN),
                 ("k", FRONT), ("m3", UNIT), ("q01", FRONT), ("pickB", TAIL), ("fxT", MLP),
                 ("q23", FRONT), ("m0", FRONT), ("v", FRONT), ("fc1", MLP)]
        USES = {"xT": "xT_used", "sx": "sx_used", "pickA": "pickA_used", "fc2": "fc2_used", "k": "kT_ready",
                "q01": "q01_used", "pickB": "pickB_used", "fxT": "fxT_used", "q23": "q23_used", "v": "v_used",
                "fc1": "fc1_used"}
        PER_ROW = {"q01": 2, "q23": 2, "v": 2}

        def use_before(t, name):
            i = [n for n, _ in FILLS].index(name) - 1
            back = 0
            while True:
                if i < 0:
                    i, back = len(FILLS) - 1, back + 1
                prev, lag = FILLS[i]
                r = t - back - lag
                if isinstance(r, int) and t - back < 0:
                    return None
                if valid(r):
                    if prev[0] == "m":
                        return "m_used", r * NE + int(prev[1]) + 1
                    return USES[prev], PER_ROW.get(prev, 1) * (r + 1)
                i -= 1

        @block.gpsimd
        def _(pool):
            count = [0]

            def const(ins):
                count[0] += 1
                ins.then_inc(sem["consts"], 1)
                pool.wait_ge(sem["consts"], count[0])

            const(nc.gpsimd.memset(eps[:], LN_EPS))
            const(nc.gpsimd.memset(quad_mask[:], 1.0))
            const(nc.gpsimd.affine_select(out=quad_mask[:], in_=quad_mask[:], compare_op=ALU.is_ge, fill=0.0, base=0,
                                          pattern=[[-32, NH]], channel_multiplier=1))
            const(nc.gpsimd.affine_select(out=quad_mask[:], in_=quad_mask[:], compare_op=ALU.is_ge, fill=0.0, base=31,
                                          pattern=[[32, NH]], channel_multiplier=-1))
            const(nc.gpsimd.memset(one_row[:], 0.0))
            for n in range(NH):
                const(nc.gpsimd.affine_select(out=one_row[:], in_=one_row[:], compare_op=ALU.not_equal, fill=1.0,
                                              base=-(32 * n + D), pattern=[[0, 1]], channel_multiplier=1))
            const(nc.gpsimd.memset(maskA[:], 0.0))
            const(nc.gpsimd.affine_select(out=maskA[:], in_=maskA[:], compare_op=ALU.is_ge, fill=MASKED, base=0,
                                          pattern=[[0, NH], [-1, P]], channel_multiplier=1))
            for i in range(2):
                const(nc.gpsimd.memset(vals[i][:], 1.0))
                const(nc.gpsimd.memset(negmax[i][:], 0.0))
                const(nc.gpsimd.memset(qm[i][:], 0.0))
            assert count[0] == CONSTS, count

            def rstds(r):
                pool.wait_ge(sem["stats_ready"], r + 1)
                nc.gpsimd.tensor_tensor(variance[:], moments[:, :, 1], eps[:], ALU.add).then_inc(sem["var_set"], 1)
                pool.wait_ge(sem["var_set"], r + 1)
                nc.gpsimd.tensor_tensor(rstd[:], variance[:], neg_half[:, 0:HALVES], ALU.pow)\
                    .then_inc(sem["rstd_ready"], 1)

            def body(t, par):
                u = (par + 0) % 2
                for e in range(NE):
                    r = t - FRONT
                    if e == 2 and valid(r):
                        pool.wait_ge(sem["kT_ready"], r + 1)
                        for dst in (kpadb, kpad):
                            nc.gpsimd.tensor_tensor(dst[1 - u][:], kT[:].unsqueeze(1).broadcast_to([128, NH, N]),
                                                    quad_mask[:].unsqueeze(2).broadcast_to([128, NH, N]), ALU.mult)\
                                .then_inc(sem["kpad_ready"], 1)
                    r = t - UNIT
                    if valid(r):
                        p = pT[e % 2]
                        pool.wait_ge(sem["t_used"], 3 * (r * NE + e) + 3)
                        pool.sem_inc(sem["settled"], 1)
                        view = p[:, 0:2, :].rearrange("p k (j n) -> p k j n", n=N)[:, :, :, 0:K0]
                        nc.gpsimd.affine_select(out=view, in_=view, compare_op=ALU.is_ge, fill=0.0, base=0,
                                                pattern=[[0, 2], [0, 2], [1, K0]], channel_multiplier=-1)\
                            .then_inc(sem["causal_done"], 1)
                        view = p[0:K1, 2, 0:NH * K1].rearrange("p (j n) -> p j n", n=K1)
                        nc.gpsimd.affine_select(out=view, in_=view, compare_op=ALU.is_ge, fill=0.0, base=0,
                                                pattern=[[0, NH], [1, K1]], channel_multiplier=-1)\
                            .then_inc(sem["causal_done"], 1)
                    r = t - LN
                    if e == 0 and valid(r):
                        rstds(r)
                    r = t - MLP
                    if e == 0 and valid(r):
                        pool.wait_ge(sem["v8_ready"], r + 1)
                        nc.gpsimd.tensor_tensor(r8[:], v8[:], neg_half[:, 0:8], ALU.pow).then_inc(sem["r8_ready"], 1)
                    r = t - FIN
                    if e == 2 and valid(r):
                        pool.wait_ge(sem["v9_ready"], r + 1)
                        nc.gpsimd.tensor_tensor(r9[:], v9[:], neg_half[:, 0:8], ALU.pow).then_inc(sem["r9_ready"], 1)
                    if e == 3 and valid(r):
                        pool.wait_ge(sem["fout_ready"], r + 1)
                        for h in range(HALVES):
                            nc.gpsimd.tensor_tensor(fprod[:, h], fout[:, h, :].unsqueeze(1).broadcast_to([P, NH, C]),
                                                    w("fgate", P).rearrange("p (n c) -> p n c", n=NH), ALU.mult)\
                                .then_inc(sem["fprod_ready"], 1)
                    r = t - TAIL
                    if e == 3 and valid(r):
                        pool.wait_ge(sem["gs_ready"], r + 1)
                        for h in range(HALVES):
                            nc.gpsimd.tensor_tensor(mixed[:, h], outs[:, h],
                                                    gate[:, h].rearrange("p n e -> p e n").unsqueeze(3)
                                                    .broadcast_to([P, NE, NH, D]), ALU.mult)\
                                .then_inc(sem["mixed_ready"], 1)

            skewed_loop(pool, body, DEPTH)

        @block.tensor
        def _(pe):
            def fill(t, name, matmuls):
                before = use_before(t, name)
                if before:
                    pe.wait_ge(sem[before[0]], before[1])
                for dst, a, m in matmuls:
                    last = nc.tensor.matmul(dst, a, m, start=True, stop=True)
                last.then_inc(sem["m_full" if name[0] == "m" else name + "_full"], 1)

            def by_halves(rows, cols, lhs, rhs):
                return [(X[0:rows, h * cols:(h + 1) * cols], lhs(h), rhs(h)) for h in range(HALVES)]

            def projections(base, par, which):
                return [(X[:, i * N:(i + 1) * N], w("ewq")[:, n * 128:(n + 1) * 128], sxT[par][:])
                        for i, n in enumerate(which)]

            def picks(par, cols):
                return [(X[0:P, i * PICK:(i + 1) * PICK], oT[par][:, i, cols], w("pick")[:, i * PICK:(i + 1) * PICK])
                        for i in range(NE)]

            def max_scores(r, par, e):
                u = r * NE + e
                if e == 0:
                    pe.wait_ge(sem["kpad_ready"], 2 * r + 1)
                    pe.wait_ge(sem["q01_used"], 2 * (r + 1))
                if e == 2:
                    pe.wait_ge(sem["q23_used"], 2 * (r + 1))
                for k in range(3):
                    need(pe, sem["r_used"], 3 * u - 2 + k)
                    if k == 0:
                        nc.tensor.matmul(R[0:P, 0, 0:4 * P], qTb[par][:, e, 0:P], kpadb[par][:, :, 0:P],
                                         start=True, stop=False)
                        nc.tensor.matmul(R[0:P, 0, 0:4 * P], identb[:], maskA[:], start=False, stop=True)\
                            .then_inc(sem["r_full"], 1)
                    else:
                        j = 2 * (k - 1)
                        nc.tensor.matmul(R[0:P, k, 0:2 * N], qTb[par][:, e, P:N], kpadb[par][:, j:j + 2, :],
                                         start=True, stop=False)
                        nc.tensor.matmul(R[0:P, k, 0:2 * N].rearrange("p (j n) -> p j n", n=N)[:, :, P:N], identb[:],
                                         maskA[:, 0:2, :], start=False, stop=True).then_inc(sem["r_full"], 1)

            def scores(r, par, e):
                u = r * NE + e
                if e == 0:
                    pe.wait_ge(sem["kpad_ready"], 2 * r + 2)
                pe.wait_ge(sem["m_used"], u + 1)
                for k in range(3):
                    need(pe, sem["t_used"], 3 * u - 2 + k)
                    for j in (range(2 * k, 2 * k + 2) if k < 2 else range(NH)):
                        if k < 2:
                            last = nc.tensor.matmul(T[:, k, (j % 2) * N:(j % 2 + 1) * N], kpad[par][:, j, 0:K0],
                                                    qm[e % 2][:], start=True, stop=True)
                        else:
                            last = nc.tensor.matmul(T[0:K1, 2, j * K1:(j + 1) * K1], kpad[par][:, j, K0:N],
                                                    qm[e % 2][:, K0:N], start=True, stop=True)
                    last.then_inc(sem["t_full"], 1)

            def weigh(r, par, e):
                u = r * NE + e
                if e == 0:
                    pe.wait_ge(sem["v_used"], 2 * (r + 1))
                pe.wait_ge(sem["causal_done"], 2 * (u + 1))
                need(pe, sem["o_used"], u)
                for s in range(2):
                    for j in range(NH):
                        if s == 0:
                            dst, src = O[32 * j:32 * j + 32, 0:N], pT[e % 2][:, j // 2, (j % 2) * N:(j % 2 + 1) * N]
                        else:
                            dst, src = O[32 * j:32 * j + 32, K0:N], pT[e % 2][0:K1, 2, j * K1:(j + 1) * K1]
                        last = nc.tensor.matmul(dst, vals[par][0:(K0, K1)[s], s, j, :], src, start=(s == 0),
                                                stop=(s == 1), tile_position=(0, 32 * j), skip_group_check=True)
                last.then_inc(sem["o_full"], 1)

            def body(t, par):
                rf, ru, rt, rm, rn = t - FRONT, t - UNIT, t - TAIL, t - MLP, t - FIN
                odd = 1 - par
                for e in range(NE):
                    nr, ne, npar = (ru, e + 1, par) if e < 3 else (rf, 0, odd)
                    if valid(nr):
                        max_scores(nr, npar, ne)
                    if valid(rf):
                        if e == 0:
                            pe.wait_ge(sem["xn_ready"], rf + 1)
                            fill(t, "xT", by_halves(C, P, lambda h: xn[:, h, :], lambda h: ident[0:P, 0:P]))
                        if e == 1:
                            pe.wait_ge(sem["xT_used"], rf + 1)
                            fill(t, "sx", [(X[:, 0:N], w("hl_t", C), xT[:])])
                        if e == 2:
                            pe.wait_ge(sem["sx_used"], rf + 1)
                            fill(t, "k", [(X[:, 0:N], w("ewk"), sxT[odd][:])])
                        if e == 3:
                            fill(t, "q23", projections(0, odd, (2, 3)))
                    if valid(ru):
                        scores(ru, par, e)
                    if valid(nr):
                        pe.wait_ge(sem["r_used"], 3 * (nr * NE + ne) + 3)
                        fill(t, f"m{ne}", by_halves(128, P, lambda h: negmax[ne % 2][:, h, :], lambda h: identb[:]))
                    if e == 0 and valid(rt):
                        weigh(rt, odd, 3)
                    if e > 0 and valid(ru):
                        weigh(ru, par, e - 1)
                    if e == 1 and valid(rt):
                        pe.wait_ge(sem["o_used"], NE * (rt + 1))
                        fill(t, "pickA", picks(odd, slice(0, P)))
                    if e == 1 and valid(rn):
                        pe.wait_ge(sem["h1m_ready"], rn + 1)
                        fill(t, "fc2", by_halves(P, C, lambda h: h1m[:, h * P:(h + 1) * P], lambda h: w("fc2", C)))
                    if e == 2 and valid(rf):
                        fill(t, "q01", projections(0, odd, (0, 1)))
                    if e == 2 and valid(rt):
                        fill(t, "pickB", picks(odd, slice(P, N)))
                    if e == 2 and valid(rm):
                        pe.wait_ge(sem["fx_ready"], rm + 1)
                        fill(t, "fxT", by_halves(C, P, lambda h: fx[par][:, h, :], lambda h: ident[0:P, 0:P]))
                    if e == 3 and valid(rf):
                        fill(t, "v", [(X[:, 0:C], sxT[odd][:, 0:K0], w("ewv")),
                                      (X[0:K1, C:2 * C], sxT[odd][:, K0:N], w("ewv"))])
                    if e == 3 and valid(rm):
                        pe.wait_ge(sem["fxT_used"], rm + 1)
                        fill(t, "fc1", [(X[:, 0:N], w("fc1", C), fxT[:])])

            pe.wait_ge(sem["consts"], CONSTS)
            skewed_loop(pe, body, DEPTH)

        @block.scalar
        def _(act):
            def used(name, dst, rows, cols, func=ACT.Copy, **kw):
                nc.scalar.activation(dst, X[rows, cols], func, **kw).then_inc(sem[name], 1)

            def body(t, par):
                rf, ru, rt, rm = t - FRONT, t - UNIT, t - TAIL, t - MLP
                odd = 1 - par
                ALL = slice(0, 128)
                for e in range(NE):
                    if valid(rf):
                        if e == 0:
                            act.wait_ge(sem["xT_full"], rf + 1)
                            used("xT_used", xT[:], slice(0, C), slice(0, N))
                        if e == 1:
                            act.wait_ge(sem["sx_full"], rf + 1)
                            need(act, sem["o_used"], NE * (rf - 1))
                            used("sx_used", sxT[odd][:], ALL, slice(0, N), ACT.Identity, bias=w("hl_bt"))
                        if e == 2:
                            act.wait_ge(sem["k_full"], rf + 1)
                            need(act, sem["kpad_ready"], 2 * rf)
                            used("kT_ready", kT[:], ALL, slice(0, N), ACT.Identity, bias=one_row[:])
                        if e == 3:
                            act.wait_ge(sem["q23_full"], rf + 1)
                            for dst in (qT, qTb):
                                used("q23_used", dst[odd][:, 2:4, :].rearrange("p a n -> p (a n)"), ALL, slice(0, 2 * N),
                                     scale=D ** 0.5)
                    if valid(ru):
                        u = ru * NE + e
                        for k in range(3):
                            act.wait_ge(sem["t_full"], 3 * u + k + 1)
                            rows, cols = (slice(0, 128), slice(0, 2 * N)) if k < 2 else (slice(0, K1), slice(0, NH * K1))
                            nc.scalar.activation(pT[e % 2][rows, k, cols], T[rows, k, cols], ACT.Exp)\
                                .then_inc(sem["t_used"], 1)
                    if e == 0 and valid(t - LAST):
                        act.wait_ge(sem["fgate_ready"], t - LAST + 1)
                        nc.scalar.activation(fexp[:], fgate[:], ACT.Exp).then_inc(sem["fexp_ready"], 1)
                    if e == 2 and valid(rf):
                        act.wait_ge(sem["q01_full"], rf + 1)
                        for dst in (qT, qTb):
                            used("q01_used", dst[odd][:, 0:2, :].rearrange("p a n -> p (a n)"), ALL, slice(0, 2 * N),
                                 scale=D ** 0.5)
                    if e == 2 and valid(rm):
                        act.wait_ge(sem["fxT_full"], rm + 1)
                        need(act, sem["h1m_ready"], rm)
                        used("fxT_used", fxT[:], slice(0, C), slice(0, N))
                    if e == 2 and valid(rt):
                        act.wait_ge(sem["gate_ready"], rt + 1)
                        nc.scalar.activation(gate_exp[:], gate[:], ACT.Exp).then_inc(sem["gexp_ready"], 1)
                    if e == 3 and valid(rf):
                        act.wait_ge(sem["v_full"], rf + 1)
                        for s, rows in enumerate((ALL, slice(0, K1))):
                            nc.scalar.activation(vals[odd][rows, s, :, 0:D],
                                                 X[rows, s * C:(s + 1) * C].rearrange("p (n d) -> p n d", n=NH), ACT.Copy)\
                                .then_inc(sem["v_used"], 1)
                    if e == 3 and valid(rm):
                        act.wait_ge(sem["fc1_full"], rm + 1)
                        used("fc1_used", h1T[:], slice(0, C), slice(0, N), ACT.Relu, bias=w("fc1_b", C))

            act.wait_ge(sem["consts"], CONSTS)
            skewed_loop(act, body, DEPTH)

        @block.vector
        def _(dve):
            steps = Steps(dve, sem["dve_step"])
            link = steps.link
            tt, ts, red = nc.vector.tensor_tensor, nc.vector.tensor_scalar, nc.vector.tensor_reduce

            def centre(z, v, ready):
                link(red(s8[:], heads(z), AX.X, ALU.add))
                link(ts(s8[:], s8[:], -1.0 / D, None, ALU.mult))
                link(tt(heads(z), heads(z), s8[:].unsqueeze(2).broadcast_to([P, HALVES * NH, D]), ALU.add))
                link(tt(sq[:], z[:], z[:], ALU.mult))
                link(red(v[:], heads(sq), AX.X, ALU.add))
                ts(v[:], v[:], 1.0 / D, LN2_EPS, ALU.mult, ALU.add).then_inc(sem[ready], 1)

            def scale_shift(dst, z, r, gamma, beta, ready):
                link(tt(heads(z), heads(z), r[:].unsqueeze(2).broadcast_to([P, HALVES * NH, D]), ALU.mult))
                link(tt(z[:], z[:], over_halves(gamma), ALU.mult))
                tt(dst[:], z[:], over_halves(beta), ALU.add).then_inc(sem[ready], 1)

            def body(t, par):
                rf, ru, rt, rm, rn, rl = t - FRONT, t - UNIT, t - TAIL, t - MLP, t - FIN, t - LAST
                odd = 1 - par
                for e in range(NE):
                    nr, ne, npar = (ru, e + 1, par) if e < 3 else (rf, 0, odd)
                    if valid(nr):
                        u = nr * NE + ne
                        for k in range(3):
                            dve.wait_ge(sem["r_full"], 3 * u + k + 1)
                            if k == 0:
                                src, dst = R[0:P, 0, 0:4 * P].rearrange("p (j s) -> p j s", j=NH), negmax[ne % 2][:, 0, D::32]
                            else:
                                src = R[0:P, k, 0:2 * N].rearrange("p (j s) -> p j s", j=2)
                                dst = negmax[ne % 2][:, 1, 64 * (k - 1) + D:64 * k:32]
                            red(dst, src, AX.X, ALU.max, negate=True).then_inc(sem["r_used"], 1)
                    if e == 0 and valid(rn):
                        dve.wait_ge(sem["fc1_used"], rn + 1)
                        nc.vector.scalar_tensor_tensor(h1m[:], fxT[:], 0.0, h1T[:], ALU.not_equal, ALU.mult)\
                            .then_inc(sem["h1m_ready"], 1)
                    if e == 0 and valid(rl):
                        dve.wait_ge(sem["fprod_ready"], HALVES * (rl + 1))
                        link(red(fgate[:], fprod[:], AX.X, ALU.add))
                        link(red(top[:, 0:HALVES], fgate[:], AX.X, ALU.max))
                        tt(fgate[:], fgate[:], top[:, 0:HALVES].unsqueeze(2).broadcast_to([P, HALVES, NH]), ALU.subtract)\
                            .then_inc(sem["fgate_ready"], 1)
                    if e == 0 and valid(rm):
                        dve.wait_ge(sem["mixed_ready"], HALVES * (rm + 1))
                        for h in range(HALVES):
                            steps.mark(red(cent[:, h, :], mixed[:, h].rearrange("p e n d -> p (n d) e"), AX.X, ALU.add))
                        steps.settle()
                        link(tt(cent[:], cent[:], residual[:], ALU.add))
                        centre(cent, v8, "v8_ready")
                    if e == 1 and valid(rl):
                        dve.wait_ge(sem["fexp_ready"], rl + 1)
                        link(red(top[:, 0:HALVES], fexp[:], AX.X, ALU.add))
                        link(nc.vector.reciprocal(top[:, 0:HALVES], top[:, 0:HALVES]))
                        link(tt(fexp[:], fexp[:], top[:, 0:HALVES].unsqueeze(2).broadcast_to([P, HALVES, NH]), ALU.mult))
                        link(tt(heads(fout), heads(fout), fexp[:].rearrange("p h n -> p (h n)").unsqueeze(2)
                                .broadcast_to([P, HALVES * NH, D]), ALU.mult))
                        link(tt(row_halves(rl), row_halves(rl), fout[:], ALU.add))
                    if e == 1 and valid(rm):
                        dve.wait_ge(sem["r8_ready"], rm + 1)
                        scale_shift(fx[par], cent, r8, "ln_g", "ln_b", "fx_ready")
                    if e == 2 and valid(rn):
                        centre(hx, v9, "v9_ready")
                    if e == 3 and valid(rt):
                        dve.wait_ge(sem["gexp_ready"], rt + 1)
                        flat = gate_exp[:].rearrange("p h n e -> p (h n) e")
                        link(red(top[:], flat, AX.X, ALU.add))
                        link(nc.vector.reciprocal(top[:], top[:]))
                        tt(gate[:].rearrange("p h n e -> p (h n) e"), flat,
                           top[:].unsqueeze(2).broadcast_to([P, HALVES * NH, NE]), ALU.mult).then_inc(sem["gs_ready"], 1)
                    if e == 3 and valid(rn):
                        dve.wait_ge(sem["r9_ready"], rn + 1)
                        scale_shift(fout, hx, r9, "fn_g", "fn_b", "fout_ready")
                    if e == 0 and valid(t):
                        for h in range(HALVES):
                            last = nc.vector.bn_stats(stats[:, h, :], stream[:, t * HALVES + h, :])
                        last.then_inc(sem["stats_set"], 1)
                        dve.wait_ge(sem["stats_set"], t + 1)
                        dve.sem_inc(sem["aggregate"], 1)
                        for h in range(HALVES):
                            last = nc.vector.bn_aggr(moments[:, h, :], stats[:, h, :])
                        last.then_inc(sem["stats_ready"], 1)
                    if valid(nr):
                        dve.wait_ge(sem["m_full"], u + 1)
                        tt(qm[ne % 2][:], X[:, 0:N], qT[npar][:, ne, :], ALU.add).then_inc(sem["m_used"], 1)
                    if e == 2 and valid(t):
                        dve.wait_ge(sem["rstd_ready"], t + 1)
                        need(dve, sem["xT_full"], t)
                        for h in range(HALVES):
                            last = ts(xn[:, h, :], stream[:, t * HALVES + h, :], moments[:, h, 0:1], rstd[:, h:h + 1],
                                      ALU.subtract, ALU.mult)
                        last.then_inc(sem["xn_ready"], 1)
                    pr, pe_, ppar = (rt, 3, odd) if e == 0 else (ru, e - 1, par)
                    if valid(pr):
                        dve.wait_ge(sem["o_full"], pr * NE + pe_ + 1)
                        nc.vector.scalar_tensor_tensor(oT[ppar][:, pe_, :], sxT[ppar][:], 0.0, O[:, 0:N], ALU.not_equal,
                                                       ALU.mult).then_inc(sem["o_used"], 1)
                    if e in (1, 2) and valid(rt):
                        h, name = e - 1, "pickA" if e == 1 else "pickB"
                        dve.wait_ge(sem[name + "_full"], rt + 1)
                        pick = X[0:P, 0:NE * PICK].rearrange("p (e c) -> p e c", e=NE)
                        link(nc.vector.reciprocal(rec[:, h], pick[:, :, C:C + NH]))
                        link(tt(glog[:, h], pick[:, :, C + NH:PICK].rearrange("p e (n f) -> p e n f", n=NH),
                                rec[:, h].unsqueeze(3).broadcast_to([P, NE, NH, NE]), ALU.mult))
                        tt(outs[:, h], pick[:, :, 0:C].rearrange("p e (n d) -> p e n d", n=NH),
                           rec[:, h].unsqueeze(3).broadcast_to([P, NE, NH, D]), ALU.mult).then_inc(sem[name + "_used"], 1)
                    if e == 2 and valid(rt):
                        flat = gate[:].rearrange("p h n f -> p h (n f)")
                        link(red(flat, glog[:].rearrange("p h e n f -> p h (n f) e"), AX.X, ALU.add))
                        link(tt(flat, flat, over_halves("gate_b"), ALU.add))
                        flat = gate[:].rearrange("p h n f -> p (h n) f")
                        link(red(top[:], flat, AX.X, ALU.max))
                        tt(flat, flat, top[:].unsqueeze(2).broadcast_to([P, HALVES * NH, NE]), ALU.subtract)\
                            .then_inc(sem["gate_ready"], 1)
                    if e == 1 and valid(rn):
                        dve.wait_ge(sem["fc2_full"], rn + 1)
                        tt(hx[:], X[0:P, 0:HALVES * C].rearrange("p (h c) -> p h c", h=HALVES), over_halves("fc2_b"), ALU.add)\
                            .then_inc(sem["fc2_used"], 1)
                        dve.wait_ge(sem["fc2_used"], rn + 1)
                        link(nc.vector.scalar_tensor_tensor(hx[:], fx[odd][:], 0.0, hx[:], ALU.not_equal, ALU.mult))
                        link(tt(hx[:], hx[:], fx[odd][:], ALU.add))

            dve.wait_ge(sem["consts"], CONSTS)
            skewed_loop(dve, body, DEPTH, steps, 2 * STEPS)


def residual_rows(env, residual):
    nc, stream, w, ident, neg_half = env["nc"], env["stream"], env["w"], env["ident"], env["neg_half"]
    with ExitStack() as ctx:
        def sb(name, shape, dt=F32):
            return ctx.enter_context(nc.sbuf_tensor("re_" + name, shape, dt))

        ROWS = NH * HALVES
        stats = sb("stats", [P, ROWS, 6])
        moments = sb("moments", [P, ROWS, 2])
        eps = sb("eps", [P, ROWS])
        rstd = sb("rstd", [P, ROWS])
        xn = sb("xn", [P, ROWS, C])
        xT = sb("xT", [C, ROWS, P])
        XT = ctx.enter_context(nc.psum_tensor("re_XT", [128, 2, 512], F32))
        SX = ctx.enter_context(nc.psum_tensor("re_SX", [128, 512], F32))
        stats_set, moments_ready, var_set, rstd_ready, xn_ready, xT_full, xT_ready, sx_full, stored = [
            ctx.enter_context(nc.semaphore("re_" + n)) for n in
            "stats_set moments_ready var_set rstd_ready xn_ready xT_full xT_ready sx_full stored".split()]
        ctx.callback(clear_semaphores, nc, [stats_set, moments_ready, var_set, rstd_ready, xn_ready, xT_full, xT_ready,
                                            sx_full, stored])
        block = ctx.enter_context(nc.Block())

        @block.vector
        def _(dve):
            for i in range(ROWS):
                nc.vector.bn_stats(stats[:, i, :], stream[:, i, :]).then_inc(stats_set, 1)
            dve.wait_ge(stats_set, ROWS)
            for i in range(ROWS):
                nc.vector.bn_aggr(moments[:, i, :], stats[:, i, :]).then_inc(moments_ready, 1)
            dve.wait_ge(rstd_ready, 1)
            for i in range(ROWS):
                nc.vector.tensor_scalar(xn[:, i, :], stream[:, i, :], moments[:, i, 0:1], rstd[:, i:i + 1], ALU.subtract,
                                        ALU.mult).then_inc(xn_ready, 1)
            dve.wait_ge(sx_full, 1)
            nc.vector.tensor_tensor(residual[:].rearrange("p h (n d) -> p n h d", n=NH),
                                    SX[0:P, 0:ROWS * D].rearrange("p (n h d) -> p n h d", n=NH, h=HALVES),
                                    w("hl_b", P).rearrange("p (n d) -> p n d", n=NH).unsqueeze(2)
                                    .broadcast_to([P, NH, HALVES, D]), ALU.add).then_inc(stored, 1)

        @block.gpsimd
        def _(pool):
            nc.gpsimd.memset(eps[:], LN_EPS).then_inc(var_set, 1)
            pool.wait_ge(moments_ready, ROWS)
            pool.wait_ge(var_set, 1)
            nc.gpsimd.tensor_tensor(eps[:], moments[:, :, 1], eps[:], ALU.add).then_inc(var_set, 1)
            pool.wait_ge(var_set, 2)
            nc.gpsimd.tensor_tensor(rstd[:], eps[:], neg_half[:, 0:ROWS], ALU.pow).then_inc(rstd_ready, 1)

        @block.tensor
        def _(pe):
            for i in range(ROWS):
                pe.wait_ge(xn_ready, i + 1)
                last = nc.tensor.matmul(XT[0:C, i // 4, (i % 4) * P:(i % 4 + 1) * P], xn[:, i, :], ident[0:P, 0:P],
                                        start=True, stop=True)
            last.then_inc(xT_full, 1)
            pe.wait_ge(xT_ready, 1)
            for i in range(ROWS):
                last = nc.tensor.matmul(SX[0:P, i * D:(i + 1) * D], xT[:, i, :],
                                        w("hl", C)[:, (i // HALVES) * D:(i // HALVES + 1) * D], start=True, stop=True)
            last.then_inc(sx_full, 1)

        @block.scalar
        def _(act):
            act.wait_ge(xT_full, 1)
            nc.scalar.activation(xT[:].rearrange("p (k i) n -> p k (i n)", k=2), XT[0:C, :, 0:4 * P], ACT.Copy)\
                .then_inc(xT_ready, 1)


def skewed_loop(eng, body, depth, steps=None, per_turn=0):
    lo = depth + 2 - depth % 2
    for t in range(lo):
        body(t, t % 2)
    turns = (B - lo) // 2
    with eng.Fori(0, turns) as i:
        if steps:
            steps.loop(i, per_turn)
        body(i * 2 + lo, 0)
        body(i * 2 + (lo + 1), 1)
    if steps:
        steps.end(turns)
    for t in range(B, B + depth):
        body(t, t % 2)


def taylor_attention(env):
    nc, stream, w = env["nc"], env["stream"], env["w"]
    ident, ones = env["ident"], env["ones"]
    DIST = TD // 2 + 1
    F = DIST * TD
    EXT = TD + TD // 2
    HC = 128 // F
    CHUNKS = [(a, min(HC, TH - a)) for a in range(0, TH, HC)]
    CH = len(CHUNKS)
    V1 = TD + 1
    with ExitStack() as ctx:
        def sb(name, shape, dt=F32):
            return ctx.enter_context(nc.sbuf_tensor("ta_" + name, shape, dt))

        def two(name, shape, dt=F32):
            return [sb(f"{name}{i}", shape, dt) for i in range(2)]

        def psum(name, dt=F32):
            return ctx.enter_context(nc.psum_tensor("ta_" + name, [128, 512], dt))

        def sem(name):
            return ctx.enter_context(nc.semaphore("ta_" + name))

        stats = sb("stats", [P, HALVES, 6])
        moments = two("moments", [P, HALVES, 2])
        std = two("std", [P, HALVES])
        rstd = sb("rstd", [P, HALVES])
        xn = two("xn", [P, HALVES, C])
        xT = two("xT", [C, N])
        qkv = two("qkv", [P, HALVES, 192])
        squares = two("squares", [P, HALVES, 128])
        v1 = two("v1_", [P, HALVES, TH, V1])
        norm2 = two("norm2", [P, HALVES * 16])
        norm = two("norm", [P, HALVES * 16])
        factor = sb("factor", [P, HALVES * 16])
        factor_of = sb("factor_of", [P, HALVES, 16])
        least = sb("least", [P, HALVES, 16])
        qkn = two("qkn", [P, HALVES, 2 * C + 1])
        ext = two("ext", [P, HALVES, 2 * TH, EXT])
        qq = two("qq", [P, HALVES, TH, DIST, TD])
        kk = two("kk", [P, HALVES, TH, DIST, TD])
        qqT = two("qqT", [HC * F, CH, N])
        qT = two("qT", [C + 1, N])
        kv2 = two("kv2", [HC * F, TH, V1])
        kv1 = two("kv1", [C + 1, TH, V1])
        mask2 = sb("mask2", [HC * F, HC, V1])
        twice = sb("twice", [HC * F, HC, V1])
        mask1 = sb("mask1", [C + 1, TH, V1])
        rec = sb("rec", [P, HALVES, TH])
        y = two("y", [P, HALVES, TH, TD])
        yT = two("yT", [C, N])
        added = sb("added", [P, HALVES, C])

        XT, QKV, KV, QQ0, QQ1, QT, Y, OUT = [psum(n) for n in ("XT", "QKV", "KV", "QQ0", "QQ1", "QT", "Y", "OUT")]

        (consts, stats_set, var_set, moments_ready, std_ready, rstd_set, xn_ready, xT_full, xT_ready, qkv_full,
         qkv_ready, squares_ready, v1_ready, norm2_ready, norm_ready, factor_set, qkn_ready, qq_ready, kk_ready,
         qqT_full, qqT_ready, kv_full, kv_ready, y_full, rec_set, y_ready, yT_full, yT_ready, out_full,
         added_set, stored, settled) = [sem(n) for n in (
             "consts stats_set var_set moments_ready std_ready rstd_set xn_ready xT_full xT_ready qkv_full "
             "qkv_ready squares_ready v1_ready norm2_ready norm_ready factor_set qkn_ready qq_ready kk_ready "
             "qqT_full qqT_ready kv_full kv_ready y_full rec_set y_ready yT_full yT_ready out_full "
             "added_set stored settled").split()]
        CONSTS = 22
        DEPTH = 8
        block = ctx.enter_context(nc.Block())

        def valid(r):
            return not isinstance(r, int) or 0 <= r < B

        def row_halves(r):
            return stream[:, bass.ds(r * HALVES, HALVES), :]

        def factors(t, h, first):
            a = t[:, h, first:first + TH, 0:TD]
            shifted = bass.AP(tensor=a.tensor, offset=a.offset, ap=[a.ap[0], a.ap[1], [1, DIST], [1, TD]])
            return a.unsqueeze(2).broadcast_to([P, TH, DIST, TD]), shifted

        @block.gpsimd
        def _(pool):
            count = [0]

            def const(ins):
                count[0] += 1
                ins.then_inc(consts, 1)
                pool.wait_ge(consts, count[0])

            const(nc.gpsimd.memset(qkn[0][:], 1.0))
            for t in (mask2, twice):
                const(nc.gpsimd.memset(t[:], 0.5))
            for t, lo, hi in ((mask2, 0, F), (twice, TD, F - TD)):
                const(nc.gpsimd.affine_select(out=t[:], in_=t[:], compare_op=ALU.is_ge, fill=0.0, base=-lo,
                                              pattern=[[-F, HC], [0, V1]], channel_multiplier=1))
                const(nc.gpsimd.affine_select(out=t[:], in_=t[:], compare_op=ALU.is_ge, fill=0.0, base=hi - 1,
                                              pattern=[[F, HC], [0, V1]], channel_multiplier=-1))
            const(nc.gpsimd.tensor_tensor(mask2[:], mask2[:], twice[:], ALU.add))
            const(nc.gpsimd.memset(mask1[:], TS2))
            const(nc.gpsimd.affine_select(out=mask1[:], in_=mask1[:], compare_op=ALU.is_ge, fill=0.0, base=0,
                                             pattern=[[-TD, TH], [0, V1]], channel_multiplier=1))
            const(nc.gpsimd.affine_select(out=mask1[:], in_=mask1[:], compare_op=ALU.is_ge, fill=0.0, base=TD - 1,
                                             pattern=[[TD, TH], [0, V1]], channel_multiplier=-1))
            for t in v1:
                const(nc.gpsimd.memset(t[:], 1.0 / N))
            const(nc.gpsimd.memset(factor_of[:], TS))
            for h in range(HALVES):
                const(nc.gpsimd.tensor_scalar(factor_of[:, h, 0:TH], w("temp", P), TS, None, ALU.mult))
            const(nc.gpsimd.memset(least[:], 1e-12))
            const(nc.gpsimd.memset(least[:, :, 0:TH], 1e-12 / TS))
            const(nc.gpsimd.memset(qkn[1][:], 1.0))
            const(nc.gpsimd.memset(qT[0][:], 1.0))
            const(nc.gpsimd.memset(qT[1][:], 1.0))
            const(nc.gpsimd.memset(mask1[C:C + 1], TS4))
            assert count[0] == CONSTS, count

            def body(t, par):
                r = t - 4
                if valid(r):
                    pool.wait_ge(qkn_ready, 3 * (r + 1))
                    need(pool, kv_full, r - 1)
                    for h in range(HALVES):
                        nc.gpsimd.tensor_tensor(kk[par][:, h], *factors(ext[par], h, TH), ALU.mult)\
                            .then_inc(kk_ready, 1)

            skewed_loop(pool, body, DEPTH)

        @block.tensor
        def _(pe):
            def body(t, par):
                r = t - 7
                p = (par + 7) % 2
                if valid(r):
                    pe.wait_ge(y_ready, r + 1)
                    need(pe, added_set, r)
                    pe.sem_inc(settled, 1)
                    for h in range(HALVES):
                        last = nc.tensor.transpose(OUT[0:C, h * P:(h + 1) * P], y[p][:, h].rearrange("p a b -> p (a b)"),
                                                   ident[0:P, 0:P])
                    last.then_inc(yT_full, 1)
                r = t - 5
                p = (par + 5) % 2
                if valid(r):
                    pe.wait_ge(qq_ready, HALVES * (r + 1))
                    need(pe, qqT_ready, 3 * r)
                    for c, (head, n) in enumerate(CHUNKS):
                        for h in range(HALVES):
                            last = nc.tensor.transpose((QQ0, QQ1)[c // 2][0:n * F, (c % 2) * N + h * P:(c % 2) * N + h * P + P],
                                                       qq[p][:, h, head:head + n].rearrange("p a d i -> p (a d i)"),
                                                       ident[0:P, 0:P])
                        if c in (1, CH - 1):
                            last.then_inc(qqT_full, 1)
                    for h in range(HALVES):
                        last = nc.tensor.transpose(QT[0:C, h * P:(h + 1) * P], qkn[p][:, h, 0:C], ident[0:P, 0:P])
                    last.then_inc(qqT_full, 1)
                    pe.wait_ge(kk_ready, HALVES * (r + 1))
                    pe.wait_ge(v1_ready, r + 1)
                    need(pe, kv_ready, 3 * r)
                    for head, n in CHUNKS:
                        for h in range(HALVES):
                            nc.tensor.matmul(KV[0:n * F, head * V1:(head + n) * V1],
                                             kk[p][:, h, head:head + n].rearrange("p a d i -> p (a d i)"),
                                             v1[p][:, h, head:head + n, :].rearrange("p a b -> p (a b)"),
                                             start=(h == 0), stop=(h == 1))
                    for h in range(HALVES):
                        last = nc.tensor.matmul(KV[0:C + 1, 128:128 + TH * V1], qkn[p][:, h, C:2 * C + 1],
                                                v1[p][:, h].rearrange("p a b -> p (a b)"), start=(h == 0), stop=(h == 1))
                    last.then_inc(kv_full, 1)
                r = t - 6
                p = (par + 6) % 2
                if valid(r):
                    pe.wait_ge(qqT_ready, 3 * (r + 1))
                    pe.wait_ge(kv_ready, 3 * (r + 1))
                    need(pe, y_ready, r)
                    for h in range(HALVES):
                        dst = Y[0:P, h * TH * V1:(h + 1) * TH * V1]
                        nc.tensor.matmul(dst, qT[p][:, h * P:(h + 1) * P], kv1[p][:].rearrange("p a b -> p (a b)"),
                                         start=True, stop=False, skip_group_check=True)
                        for c, (head, n) in enumerate(CHUNKS):
                            last = nc.tensor.matmul(dst[:, head * V1:(head + n) * V1], qqT[p][0:n * F, c, h * P:(h + 1) * P],
                                                    kv2[p][0:n * F, head:head + n, :].rearrange("p a b -> p (a b)"),
                                                    start=False, stop=(c == CH - 1), skip_group_check=True)
                    last.then_inc(y_full, 1)
                r = t - 7
                p = (par + 7) % 2
                if valid(r):
                    pe.wait_ge(yT_ready, r + 1)
                    for h in range(HALVES):
                        last = nc.tensor.matmul(OUT[0:P, 256 + h * C:256 + (h + 1) * C], yT[p][:, h * P:(h + 1) * P],
                                                w("wproj", C)[:, 0:C], start=True, stop=True)
                    last.then_inc(out_full, 1)
                r = t - 2
                p = par
                if valid(r):
                    pe.wait_ge(xT_ready, r + 1)
                    need(pe, qkv_ready, r)
                    for h in range(HALVES):
                        last = nc.tensor.matmul(QKV[0:P, h * 192:(h + 1) * 192], xT[p][:, h * P:(h + 1) * P],
                                                w("wqkv", C), start=True, stop=True)
                    last.then_inc(qkv_full, 1)
                r = t - 1
                p = (par + 1) % 2
                if valid(r):
                    pe.wait_ge(xn_ready, r + 1)
                    need(pe, xT_ready, r)
                    pe.sem_inc(settled, 1)
                    for h in range(HALVES):
                        last = nc.tensor.transpose(XT[0:C, h * P:(h + 1) * P], xn[p][:, h, :], ident[0:P, 0:P])
                    last.then_inc(xT_full, 1)

            pe.wait_ge(consts, CONSTS)
            skewed_loop(pe, body, DEPTH)

        @block.scalar
        def _(act):
            def body(t, par):
                r, p = t - 7, (par + 7) % 2
                if valid(r):
                    act.wait_ge(yT_full, r + 1)
                    nc.scalar.activation(yT[p][:], OUT[0:C, 0:N], ACT.Copy).then_inc(yT_ready, 1)
                r, p = t, par
                if valid(r):
                    act.wait_ge(moments_ready, r + 1)
                    nc.scalar.activation(std[p][:], moments[p][:, :, 1], ACT.Sqrt).then_inc(std_ready, 1)
                r, p = t - 3, (par + 3) % 2
                if valid(r):
                    act.wait_ge(norm2_ready, r + 1)
                    nc.scalar.activation(norm[p][:], norm2[p][:], ACT.Sqrt).then_inc(norm_ready, 1)
                r, p = t - 5, (par + 5) % 2
                if valid(r):
                    need(act, y_full, r - 1)
                    for i, bank in enumerate((QQ0, QQ1)):
                        act.wait_ge(qqT_full, 3 * r + i + 1)
                        c, n = 2 * i, min(2, CH - 2 * i)
                        rows = CHUNKS[c][1] * F
                        nc.scalar.activation(qqT[p][0:rows, c:c + n, :].rearrange("p a b -> p (a b)"),
                                             bank[0:rows, 0:n * N], ACT.Copy).then_inc(qqT_ready, 1)
                    act.wait_ge(qqT_full, 3 * r + 3)
                    nc.scalar.activation(qT[p][0:C], QT[0:C, 0:N], ACT.Copy).then_inc(qqT_ready, 1)
                r, p = t - 4, par
                if valid(r):
                    need(act, y_full, r - 1)
                    nc.scalar.activation(v1[p][:, :, :, 0:TD],
                                         qkv[p][:, :, 2 * C:3 * C].rearrange("p a (b c) -> p a b c", c=TD), ACT.Copy,
                                         scale=1.0 / N).then_inc(v1_ready, 1)
                r, p = t - 2, par
                if valid(r):
                    act.wait_ge(qkv_ready, r + 1)
                    nc.scalar.activation(squares[p][:], qkv[p][:, :, 0:128], ACT.Square).then_inc(squares_ready, 1)
                r, p = t - 1, (par + 1) % 2
                if valid(r):
                    act.wait_ge(xT_full, r + 1)
                    nc.scalar.activation(xT[p][:], XT[0:C, 0:N], ACT.Copy).then_inc(xT_ready, 1)

            act.wait_ge(consts, CONSTS)
            skewed_loop(act, body, DEPTH)

        @block.vector
        def _(dve):
            def body(t, par):
                r, p = t - 1, (par + 1) % 2
                if valid(r):
                    dve.wait_ge(std_ready, r + 1)
                    nc.vector.reciprocal(rstd[:], std[p][:]).then_inc(rstd_set, 1)
                    dve.wait_ge(rstd_set, r + 1)
                    for h in range(HALVES):
                        last = nc.vector.tensor_scalar(xn[p][:, h, :], stream[:, r * HALVES + h, :], moments[p][:, h, 0:1],
                                                       rstd[:, h:h + 1], ALU.subtract, ALU.mult)
                    last.then_inc(xn_ready, 1)
                r, p = t, par
                if valid(r):
                    for h in range(HALVES):
                        nc.vector.bn_stats(stats[:, h, :], stream[:, r * HALVES + h, :]).then_inc(stats_set, 1)
                    dve.wait_ge(stats_set, HALVES * (r + 1))
                    dve.sem_inc(var_set, 1)
                    for h in range(HALVES):
                        last = nc.vector.bn_aggr(moments[p][:, h, :], stats[:, h, :])
                    last.then_inc(var_set, 1)
                    dve.wait_ge(var_set, 2 * (r + 1))
                    nc.vector.tensor_scalar(moments[p][:, :, 1], moments[p][:, :, 1], LN_EPS, None, ALU.add)\
                        .then_inc(moments_ready, 1)
                r, p = t - 3, (par + 3) % 2
                if valid(r):
                    dve.wait_ge(squares_ready, r + 1)
                    nc.vector.tensor_reduce(norm2[p][:], squares[p][:].rearrange("p h (a d) -> p (h a) d", d=TD), AX.X,
                                            ALU.add).then_inc(norm2_ready, 1)
                r, p = t - 4, par
                if valid(r):
                    dve.wait_ge(norm_ready, r + 1)
                    nc.vector.tensor_tensor(factor[:], norm[p][:], least[:].rearrange("p a b -> p (a b)"), ALU.max)\
                        .then_inc(factor_set, 1)
                    dve.wait_ge(factor_set, 3 * r + 1)
                    nc.vector.reciprocal(factor[:], factor[:]).then_inc(factor_set, 1)
                    dve.wait_ge(factor_set, 3 * r + 2)
                    nc.vector.tensor_tensor(factor[:], factor[:], factor_of[:].rearrange("p a b -> p (a b)"), ALU.mult)\
                        .then_inc(factor_set, 1)
                    dve.wait_ge(factor_set, 3 * r + 3)
                    parts = qkv[p][:, :, 0:128].rearrange("p h (a d) -> p h a d", d=TD)
                    for dst, n in ((ext[p][:, :, :, 0:TD], TD), (ext[p][:, :, :, TD:EXT], EXT - TD),
                                   (qkn[p][:, :, 0:2 * C].rearrange("p h (a d) -> p h a d", d=TD), TD)):
                        nc.vector.tensor_tensor(dst, parts[:, :, :, 0:n],
                                                factor[:].rearrange("p (h a) -> p h a", h=HALVES).unsqueeze(3)
                                                .broadcast_to([P, HALVES, 2 * TH, n]), ALU.mult).then_inc(qkn_ready, 1)
                    dve.wait_ge(qkn_ready, 3 * (r + 1))
                    for h in range(HALVES):
                        nc.vector.tensor_tensor(qq[p][:, h], *factors(ext[p], h, 0), ALU.mult)\
                            .then_inc(qq_ready, 1)
                r, p = t - 5, (par + 5) % 2
                if valid(r):
                    dve.wait_ge(kv_full, r + 1)
                    for head, rows, n in ((0, HC * F, TH // HC * HC), (TH // HC * HC, TH % HC * F, TH % HC)):
                        m = mask2[0:rows, 0:min(n, HC)].rearrange("p a b -> p (a b)")
                        nc.vector.tensor_tensor(
                            kv2[p][0:rows, head:head + n].rearrange("p (c a) b -> p c (a b)", a=min(n, HC)),
                            KV[0:rows, head * V1:(head + n) * V1].rearrange("p (c a) -> p c a", a=min(n, HC) * V1),
                            m.unsqueeze(1).broadcast_to([rows, max(1, n // HC), min(n, HC) * V1]), ALU.mult)\
                            .then_inc(kv_ready, 1)
                    nc.vector.tensor_tensor(kv1[p][:], KV[0:C + 1, 128:128 + TH * V1].rearrange("p (a b) -> p a b", a=TH),
                                            mask1[:], ALU.mult).then_inc(kv_ready, 1)
                r, p = t - 6, (par + 6) % 2
                if valid(r):
                    dve.wait_ge(y_full, r + 1)
                    Yv = Y[0:P, 0:HALVES * TH * V1].rearrange("p (a b c) -> p a b c", a=HALVES, b=TH)
                    nc.vector.reciprocal(rec[:], Yv[:, :, :, TD]).then_inc(rec_set, 1)
                    dve.wait_ge(rec_set, r + 1)
                    nc.vector.tensor_tensor(y[p][:], Yv[:, :, :, 0:TD], rec[:].unsqueeze(3).broadcast_to([P, HALVES, TH, TD]),
                                            ALU.mult).then_inc(y_ready, 1)
                r, p = t - 2, par
                if valid(r):
                    dve.wait_ge(qkv_full, r + 1)
                    need(dve, v1_ready, r - 1)
                    nc.vector.tensor_tensor(qkv[p][:], QKV[0:P, 0:HALVES * 192].rearrange("p (h c) -> p h c", h=HALVES),
                                            w("bqkv", P).unsqueeze(1).broadcast_to([P, HALVES, 192]), ALU.add)\
                        .then_inc(qkv_ready, 1)
                r, p = t - 7, (par + 7) % 2
                if valid(r):
                    dve.wait_ge(out_full, r + 1)
                    need(dve, stored, r)
                    nc.vector.tensor_tensor(added[:], OUT[0:P, 256:256 + HALVES * C].rearrange("p (h c) -> p h c", h=HALVES),
                                            w("bproj", P).unsqueeze(1).broadcast_to([P, HALVES, C]), ALU.add)\
                        .then_inc(added_set, 1)
                r = t - 7
                if valid(r):
                    dve.wait_ge(added_set, r + 1)
                    nc.vector.tensor_tensor(row_halves(r), row_halves(r), added[:], ALU.add).then_inc(stored, 1)

            dve.wait_ge(consts, CONSTS)
            skewed_loop(dve, body, DEPTH)


def mixture(env):
    nc, stream, w = env["nc"], env["stream"], env["w"]
    ident, identb, neg_half, w_parts = env["ident"], env["identb"], env["neg_half"], env["w_parts"]
    PAIRS = ((0, 0), (0, 1), (1, 2))
    with ExitStack() as ctx:
        def sb(name, shape, dt=F32):
            return ctx.enter_context(nc.sbuf_tensor("mo_" + name, shape, dt))

        def two(name, shape, dt=F32):
            return [sb(f"{name}{i}", shape, dt) for i in range(2)]

        def psum(name, dt=F32):
            return ctx.enter_context(nc.psum_tensor("mo_" + name, [128, 2048 // mybir.dt.size(dt)], dt))

        stats = sb("stats", [P, HALVES, 6])
        moments = [sb(f"moments{i}", [P, HALVES, 2]) for i in range(2)]
        var = two("var", [P, HALVES])
        rstd = two("rstd", [P, HALVES])
        xn = sb("xn", [P, HALVES, C])
        xg = two("xg", [P, HALVES, C])
        xs = two("xs", [P, HALVES, 4, C], BF16)
        rest = two("rest", [P, HALVES, C])
        xT = two("xT", [128, 2, N], BF16)
        hT = two("hT", [HID, E, N])
        logits = sb("logits", [P, HALVES, E])
        best = two("best", [P, HALVES, E])
        which = sb("which", [P, HALVES, E], U32)
        whichf = two("whichf", [P, HALVES, 2])
        behind = two("behind", [P, HALVES])
        half_tanh = two("half_tanh", [P, HALVES])
        share = sb("share", [P, HALVES, 2])
        number = sb("number", [P, E])
        pick = sb("pick", [P, 2, HALVES, E])
        gate = two("gate", [P, HALVES, E])
        gateT = two("gateT", [E, N])
        weighted = sb("weighted", [P, HALVES, E, C])
        mixed = sb("mixed", [P, HALVES, C])

        XT = psum("XT", BF16)
        LG, GT, B2, H0, H1, Y0, Y1 = [psum(n) for n in "LG GT B2 H0 H1 Y0 Y1".split()]
        HB, YB = (H0, H1), (Y0, Y1)
        names = ("consts stats_set stats_settled moments_ready var_ready rstd_ready xn_set xg_ready xT_full xT_ready "
                 "h_full h_ready logits_full logits_set best_set behind_ready tanh_ready whichf_ready share_set "
                 "pick_set gate_ready y_full y_used weighted_set mixed_set gateT_full gateT_ready b2_full b2_used stored parts_ready fence").split()
        (consts, stats_set, stats_settled, moments_ready, var_ready, rstd_ready, xn_set, xg_ready, xT_full, xT_ready,
         h_full, h_ready, logits_full, logits_set, best_set, behind_ready, tanh_ready, whichf_ready, share_set,
         pick_set, gate_ready, y_full, y_used, weighted_set, mixed_set, gateT_full, gateT_ready, b2_full,
         b2_used, stored, parts_ready, fence) = [ctx.enter_context(nc.semaphore("mo_" + n)) for n in names]
        DEPTH = 8
        block = ctx.enter_context(nc.Block())

        def valid(r):
            return not isinstance(r, int) or 0 <= r < B

        def row_halves(r):
            return stream[:, bass.ds(r * HALVES, HALVES), :]

        def over_halves(name):
            return w(name, P).unsqueeze(1).broadcast_to([P, HALVES, w(name, P).shape[1]])

        @block.gpsimd
        def _(pool):
            nc.gpsimd.iota(number[:], pattern=[[1, E]], base=0, channel_multiplier=0,
                           allow_small_or_imprecise_dtypes=True).then_inc(consts, 1)

            def body(t, par):
                r, p = t - 1, 1 - par
                if valid(r):
                    pool.wait_ge(var_ready, r + 1)
                    need(pool, xn_set, 2 * (r - 1))
                    nc.gpsimd.tensor_tensor(rstd[p][:], var[p][:], neg_half[:, 0:HALVES], ALU.pow)\
                        .then_inc(rstd_ready, 1)
                r, p = t - 3, 1 - par
                if valid(r):
                    pool.wait_ge(xg_ready, r + 1)
                    need(pool, xT_full, r - 1)
                    pool.sem_inc(fence, 1)
                    nc.gpsimd.tensor_copy(xs[p][:, :, 0], xg[p][:]).then_inc(parts_ready, 1)
                    nc.gpsimd.tensor_copy(xs[p][:, :, 2], xg[p][:]).then_inc(parts_ready, 1)
                    pool.wait_ge(parts_ready, 5 * r + 2)
                    nc.gpsimd.tensor_tensor(rest[p][:], xg[p][:], xs[p][:, :, 0], ALU.subtract).then_inc(parts_ready, 1)
                    pool.wait_ge(parts_ready, 5 * r + 3)
                    pool.sem_inc(fence, 1)
                    nc.gpsimd.tensor_copy(xs[p][:, :, 1], rest[p][:]).then_inc(parts_ready, 1)
                    pool.wait_ge(parts_ready, 5 * r + 4)
                    nc.gpsimd.tensor_tensor(xs[p][:, :, 3], rest[p][:], xs[p][:, :, 1], ALU.subtract)\
                        .then_inc(parts_ready, 1)

            skewed_loop(pool, body, DEPTH)

        @block.tensor
        def _(pe):
            def body(t, par):
                r, p = t - 6, par
                if valid(r):
                    for h in range(HALVES):
                        pe.wait_ge(h_ready, E * (r + 1))
                        need(pe, y_used, HALVES * r)
                        for e in range(E):
                            last = nc.tensor.matmul(YB[h][0:P, e * C:(e + 1) * C], hT[p][:, e, h * P:(h + 1) * P],
                                                    w("w2")[:, e * C:(e + 1) * C], start=True, stop=True)
                        last.then_inc(y_full, 1)
                r, p = t - 8, par
                if valid(r):
                    pe.wait_ge(gateT_ready, r + 1)
                    need(pe, b2_used, r)
                    for h in range(HALVES):
                        last = nc.tensor.matmul(B2[0:P, h * C:(h + 1) * C], gateT[p][:, h * P:(h + 1) * P],
                                                w("b2", E), start=True, stop=True)
                    last.then_inc(b2_full, 1)
                r, p = t - 4, par
                if valid(r):
                    pe.wait_ge(xT_ready, r + 1)
                    need(pe, logits_set, r)
                    for h in range(HALVES):
                        for n, (a, b) in enumerate(PAIRS):
                            last = nc.tensor.matmul(LG[0:P, h * E:(h + 1) * E], xT[p][:, a, h * P:(h + 1) * P],
                                                    w_parts[:, b, E * HID:E * HID + E], start=(n == 0), stop=(n == 2))
                    last.then_inc(logits_full, 1)
                    for e in range(E):
                        if e % 2 == 0:
                            need(pe, h_ready, E * r + e - 2)
                        for n, (a, b) in enumerate(PAIRS):
                            last = nc.tensor.matmul(HB[e // 2 % 2][:, (e % 2) * N:(e % 2 + 1) * N],
                                                    w_parts[:, b, e * HID:(e + 1) * HID], xT[p][:, a, :],
                                                    start=(n == 0), stop=(n == 2))
                        if e % 2:
                            last.then_inc(h_full, 1)
                r, p = t - 7, 1 - par
                if valid(r):
                    pe.wait_ge(gate_ready, r + 1)
                    need(pe, gateT_ready, r)
                    for h in range(HALVES):
                        last = nc.tensor.matmul(GT[0:E, h * P:(h + 1) * P], gate[p][:, h, :], ident[0:P, 0:P],
                                                start=True, stop=True)
                    last.then_inc(gateT_full, 1)
                r, p = t - 3, 1 - par
                if valid(r):
                    pe.wait_ge(parts_ready, 5 * (r + 1))
                    need(pe, xT_ready, r)
                    for k in range(2):
                        for h in range(HALVES):
                            last = nc.tensor.transpose(XT[:, k * N + h * P:k * N + (h + 1) * P],
                                                       xs[p][:, h, 2 * k:2 * k + 2, :].rearrange("p a c -> p (a c)"),
                                                       identb[:])
                    last.then_inc(xT_full, 1)

            skewed_loop(pe, body, DEPTH)

        @block.scalar
        def _(act):
            def body(t, par):
                r, p = t - 5, 1 - par
                if valid(r):
                    act.wait_ge(behind_ready, r + 1)
                    need(act, share_set, r - 1)
                    nc.scalar.activation(half_tanh[p][:], behind[p][:], ACT.Tanh, scale=0.5).then_inc(tanh_ready, 1)
                r, p = t - 4, par
                if valid(r):
                    need(act, y_full, HALVES * (r - 1))
                    for e in range(E):
                        if e % 2 == 0:
                            act.wait_ge(h_full, E // 2 * r + e // 2 + 1)
                        nc.scalar.activation(hT[p][:, e, :], HB[e // 2 % 2][:, (e % 2) * N:(e % 2 + 1) * N], ACT.Gelu,
                                             bias=w("b1")[:, e:e + 1]).then_inc(h_ready, 1)
                r, p = t - 7, 1 - par
                if valid(r):
                    act.wait_ge(gateT_full, r + 1)
                    need(act, b2_full, r - 1)
                    nc.scalar.activation(gateT[p][:], GT[0:E, 0:N], ACT.Copy).then_inc(gateT_ready, 1)
                r, p = t - 3, 1 - par
                if valid(r):
                    act.wait_ge(xT_full, r + 1)
                    need(act, h_full, E // 2 * (r - 1))
                    nc.scalar.activation(xT[p][:].rearrange("p a n -> p (a n)"), XT[:, 0:2 * N], ACT.Copy)\
                        .then_inc(xT_ready, 1)

            skewed_loop(act, body, DEPTH)

        @block.vector
        def _(dve):
            def body(t, par):
                r, p = t - 6, par
                if valid(r):
                    dve.wait_ge(tanh_ready, r + 1)
                    for k, sign in ((0, -0.5), (1, 0.5)):
                        last = nc.vector.tensor_scalar(share[:, :, k], half_tanh[p][:], sign, 0.5, ALU.mult, ALU.add)
                    last.then_inc(share_set, 1)
                    dve.wait_ge(share_set, r + 1)
                    for k in range(2):
                        for h in range(HALVES):
                            last = nc.vector.tensor_scalar(pick[:, k, h, :], number[:], whichf[p][:, h, k:k + 1],
                                                           share[:, h, k:k + 1], ALU.is_equal, ALU.mult)
                    last.then_inc(pick_set, 1)
                    dve.wait_ge(pick_set, r + 1)
                    need(dve, gateT_full, r - 1)
                    nc.vector.tensor_tensor(gate[p][:], pick[:, 0], pick[:, 1], ALU.add).then_inc(gate_ready, 1)
                r, p = t - 5, 1 - par
                if valid(r):
                    dve.wait_ge(logits_full, r + 1)
                    nc.vector.tensor_tensor(logits[:], LG[0:P, 0:HALVES * E].rearrange("p (h e) -> p h e", h=HALVES),
                                            over_halves("br"), ALU.add).then_inc(logits_set, 1)
                    dve.wait_ge(logits_set, r + 1)
                    dve.sem_inc(stats_settled, 1)
                    for h in range(HALVES):
                        last = nc.vector.max(best[p][:, h, :], logits[:, h, :])
                    last.then_inc(best_set, 1)
                    dve.wait_ge(best_set, 2 * r + 1)
                    need(dve, tanh_ready, r - 1)
                    nc.vector.tensor_tensor(behind[p][:], best[p][:, :, 1], best[p][:, :, 0], ALU.subtract)\
                        .then_inc(behind_ready, 1)
                    for h in range(HALVES):
                        last = nc.vector.max_index(which[:, h, :], best[p][:, h, :], logits[:, h, :])
                    last.then_inc(best_set, 1)
                    dve.wait_ge(best_set, 2 * r + 2)
                    nc.vector.tensor_copy(whichf[p][:], which[:, :, 0:2]).then_inc(whichf_ready, 1)
                r, p = t - 6, par
                if valid(r):
                    dve.wait_ge(gate_ready, r + 1)
                    for h in range(HALVES):
                        dve.wait_ge(y_full, HALVES * r + h + 1)
                        nc.vector.tensor_tensor(weighted[:, h], YB[h][0:P, :].rearrange("p (e c) -> p e c", e=E),
                                                gate[p][:, h, :].unsqueeze(2).broadcast_to([P, E, C]), ALU.mult)\
                            .then_inc(y_used, 1)
                r, p = t - 8, par
                if valid(r):
                    dve.wait_ge(b2_full, r + 1)
                    nc.vector.tensor_tensor(row_halves(r), row_halves(r),
                                            B2[0:P, 0:HALVES * C].rearrange("p (h c) -> p h c", h=HALVES),
                                            ALU.add).then_inc(b2_used, 1)
                r, p = t - 6, par
                if valid(r):
                    dve.wait_ge(y_used, HALVES * (r + 1))
                    for h in range(HALVES):
                        last = nc.vector.tensor_reduce(mixed[:, h, :], weighted[:, h].rearrange("p e c -> p c e"), AX.X, ALU.add)
                    last.then_inc(mixed_set, 1)
                    dve.wait_ge(mixed_set, r + 1)
                    nc.vector.tensor_tensor(row_halves(r), row_halves(r), mixed[:], ALU.add).then_inc(stored, 1)
                r, p = t - 2, par
                if valid(r):
                    dve.wait_ge(rstd_ready, r + 1)
                    for h in range(HALVES):
                        last = nc.vector.tensor_scalar(xn[:, h, :], stream[:, r * HALVES + h, :], moments[p][:, h, 0:1],
                                                       rstd[p][:, h:h + 1], ALU.subtract, ALU.mult)
                    last.then_inc(xn_set, 1)
                    dve.wait_ge(xn_set, 2 * r + 1)
                    nc.vector.tensor_tensor(xn[:], xn[:], over_halves("gamma"), ALU.mult).then_inc(xn_set, 1)
                    dve.wait_ge(xn_set, 2 * r + 2)
                    need(dve, parts_ready, 5 * (r - 1))
                    nc.vector.tensor_tensor(xg[p][:], xn[:], over_halves("beta"), ALU.add).then_inc(xg_ready, 1)
                r, p = t, par
                if valid(r):
                    for h in range(HALVES):
                        last = nc.vector.bn_stats(stats[:, h, :], stream[:, r * HALVES + h, :])
                    last.then_inc(stats_set, 1)
                    dve.wait_ge(stats_set, r + 1)
                    dve.sem_inc(stats_settled, 1)
                    for h in range(HALVES):
                        last = nc.vector.bn_aggr(moments[p][:, h, :], stats[:, h, :])
                    last.then_inc(moments_ready, 1)
                    dve.wait_ge(moments_ready, r + 1)
                    need(dve, rstd_ready, r - 1)
                    nc.vector.tensor_scalar(var[p][:], moments[p][:, :, 1], 1.0 + LN_EPS, LN_EPS * LN_EPS, ALU.mult,
                                            ALU.add).then_inc(var_ready, 1)

            dve.wait_ge(consts, 1)
            skewed_loop(dve, body, DEPTH)


def write_out(env, out):
    nc, stream = env["nc"], env["stream"]
    with ExitStack() as ctx:
        written = ctx.enter_context(nc.semaphore("written"))
        block = ctx.enter_context(nc.Block())

        @block.sync
        def _(sp):
            o = out.rearrange("b (h p) c -> h p b c", h=HALVES)
            for h in range(HALVES):
                sp.dma_start(o[h], stream[:, h:TILES:HALVES, :]).then_inc(written, 16)
            sp.wait_ge(written, 16 * HALVES)


def lay_out(a):
    big = np.zeros((128, W_COLS), np.float32)

    def at(name):
        s, n = WEIGHTS[name]
        return big[:, s:s + n]

    def rows(name, v):
        at(name)[:, :] = np.broadcast_to(np.reshape(v, (1, -1)), (128, v.size))

    rows("conv", a["L0_tok_w"])
    rows("conv_b", a["L0_tok_b"])
    rows("tok_gamma", a["L0_tok_gamma"])
    rows("tok_beta", a["L0_tok_beta"])
    rows("tok_alpha", a["L0_tok_alpha"])
    for dst, src in (("wq", "Wq"), ("wk", "Wk"), ("wv", "Wv")):
        at(dst)[0:C] = a["L0_attn_" + src]
    for g in range(2):
        at("wo")[:, g * C:(g + 1) * C] = a["L0_attn_Wo"][g * 128:(g + 1) * 128]
    rows("bo", a["L0_attn_bo"])
    at("hl_bt")[:, 0] = 1.0
    for n in range(NH):
        r, c = slice(32 * n, 32 * n + D), slice(D * n, D * n + D)
        at("hl_t")[0:C, r] = a["L0_ffn_hl_w"][n].T
        at("hl_bt")[r, 0] = a["L0_ffn_hl_b"][n]
        at("hl")[0:C, c] = a["L0_ffn_hl_w"][n].T
        at("ewk")[r, r] = a["L0_ffn_wk"][n].T
        at("ewv")[r, c] = a["L0_ffn_wv"][n].T
        at("fc1")[c, c] = a["L0_ffn_fc1_w"].T
        at("fc2")[c, c] = a["L0_ffn_fc2_w"].T
        at("fc1_b")[c, 0] = a["L0_ffn_fc1_b"]
        for e in range(NE):
            at("ewq")[r, 128 * e + 32 * n:128 * e + 32 * n + D] = a["L0_ffn_wq"][n, e].T
            pick = at("pick")[:, 84 * e:84 * (e + 1)]
            pick[r, c] = np.eye(D, dtype=np.float32)
            pick[32 * n + D, C + n] = 1.0
            pick[r, 68 + 4 * n:72 + 4 * n] = a["L0_ffn_gate_w"][n, :, e * D:(e + 1) * D].T
    rows("hl_b", a["L0_ffn_hl_b"])
    rows("gate_b", a["L0_ffn_gate_b"])
    for dst, src in (("ln_g", "ln_g"), ("ln_b", "ln_b"), ("fc2_b", "fc2_b"), ("fn_g", "fnorm_g"),
                     ("fn_b", "fnorm_b")):
        rows(dst, np.tile(a["L0_ffn_" + src], NH))
    rows("fgate", a["L0_ffn_fgate_w"])
    at("wproj")[0:C, 0:C] = a["L1_attn_Wproj"].T
    at("wqkv")[0:C] = a["L1_attn_Wqkv"].T
    rows("bqkv", a["L1_attn_bqkv"])
    rows("bproj", a["L1_attn_bproj"])
    rows("temp", a["L1_attn_temperature"])
    rows("gamma", a["L1_ffn_gamma"])
    rows("beta", a["L1_ffn_beta"])
    for half in (slice(0, C), slice(C, 2 * C)):
        at("wr")[half] = a["L1_ffn_Wr"]
    rows("br", a["L1_ffn_br"])
    for e in range(E):
        for half in (slice(0, C), slice(C, 2 * C)):
            at("w1")[half, e * HID:(e + 1) * HID] = a["L1_ffn_W1"][e]
        at("b1")[:, e] = a["L1_ffn_b1"][e]
        at("w2")[:, e * C:(e + 1) * C] = a["L1_ffn_W2"][e]
    at("b2")[0:E] = a["L1_ffn_b2"]
    return big


def kernel(**inputs):
    import numpy as _np
    import concourse.bacc as _bacc
    from concourse.bass_utils import run_bass_kernel_spmd as _run

    arrays = {k: _np.asarray(v) for k, v in inputs.items()}
    x_pad = _np.zeros((B, T_IN + 2 * PAD, C), _np.float32)
    x_pad[:, PAD:PAD + T_IN] = arrays["x"]
    ins = {"x_pad": x_pad, "weights": lay_out(arrays)}
    nc = _bacc.Bacc("TRN2", target_bir_lowering=False, num_devices=1)
    args = [nc.dram_tensor(k, v.shape, F32, kind="ExternalInput").ap() for k, v in ins.items()]
    out = nc.dram_tensor("out", (B, N, C), F32, kind="ExternalOutput").ap()
    build(nc, *args, out)
    return _run(nc, [ins], core_ids=[0]).results[0]["out"]
```
